# Optimizing a Trainium2 kernel written in Bass

```python
import numpy as np
import jax
import jax.numpy as jnp

def _softmax(x, axis=-1):
    return jax.nn.softmax(x, axis=axis)
def _gelu(x):
    return jax.nn.gelu(x, approximate=True)
def _silu(x):
    return jax.nn.silu(x)
def _sigmoid(x):
    return jax.nn.sigmoid(x)
def _layernorm(x, axis=-1, eps=1e-5):
    m = jnp.mean(x, axis=axis, keepdims=True)
    v = jnp.var(x, axis=axis, keepdims=True)
    return (x - m) / jnp.sqrt(v + eps)
def _scatter_add(tgt, idx, src, axis=0):
    return tgt.at[idx].add(src)
def _segment_sum(src, seg, n):
    return jax.ops.segment_sum(src, seg, n)

kernel_name = 'mk_conv_seq_d1_conv_nhwc192_7ff0d2'

def setup_inputs(seed: int = 0):
    np.random.seed(seed)
    _w = jnp.asarray
    def _rec_inputs():
        import jax
        import jax.numpy as jnp
        _gk = jax.random.key(seed)
        x = -0.0004039 + 1 * jax.random.normal(jax.random.fold_in(_gk, 1), (16, 64, 64, 192), jnp.float32)
        return x
    x = _rec_inputs()
    def _L0_conv_setup():
        import jax, jax.numpy as jnp
        import numpy as np
        B, H, W, C = (16, 64, 64, 192)
        HEAD_DIM, N_HEADS, P = (32, 6, 8)
        SHIFT = P // 2
        EPS = 1e-05

        def _layernorm(x, g, b):
            mu = jnp.mean(x, -1, keepdims=True)
            var = jnp.mean((x - mu) ** 2, -1, keepdims=True)
            return (x - mu) * jax.lax.rsqrt(var + EPS) * g + b

        def _rel_bias(rel_pos):
            coords = np.stack(np.meshgrid(np.arange(P), np.arange(P), indexing='ij'), -1).reshape(-1, 2)
            rel = coords[:, None] - coords[None, :] + P - 1
            return rel_pos[:, rel[..., 0], rel[..., 1]]

        def _shift_mask():
            hw, ww = (H // P, W // P)
            m = np.zeros((hw, ww, P, P, P, P), dtype=bool)
            s = P - SHIFT
            m[-1, :, :s, :, s:, :] = True
            m[-1, :, s:, :, :s, :] = True
            m[:, -1, :, :s, :, s:] = True
            m[:, -1, :, s:, :, :s] = True
            return m.reshape(hw * ww, P * P, P * P)
        key = jax.random.key(seed)
        ks = jax.random.split(key, 8)
        f32 = jnp.float32
        rn = lambda k, shape: jax.random.normal(k, shape, f32) * 0.02
        return {'x': jax.random.normal(ks[0], (B, H, W, C), f32), 'g1': jnp.ones((C,), f32), 'b1': jnp.zeros((C,), f32), 'w_qkv': rn(ks[1], (C, 3 * C)), 'b_qkv': jnp.zeros((3 * C,), f32), 'rel_pos': rn(ks[2], (N_HEADS, 2 * P - 1, 2 * P - 1)), 'w_proj': rn(ks[3], (C, C)), 'b_proj': jnp.zeros((C,), f32), 'g2': jnp.ones((C,), f32), 'b2': jnp.zeros((C,), f32), 'w_mlp1': rn(ks[4], (C, 4 * C)), 'b_mlp1': jnp.zeros((4 * C,), f32), 'w_mlp2': rn(ks[5], (4 * C, C)), 'b_mlp2': jnp.zeros((C,), f32)}
    _L0_conv_all = _L0_conv_setup()
    _L0_conv_in = {k: v for k, v in _L0_conv_all.items() if k in ('g1', 'b1', 'w_qkv', 'b_qkv', 'rel_pos', 'w_proj', 'b_proj', 'g2', 'b2', 'w_mlp1', 'b_mlp1', 'w_mlp2', 'b_mlp2', )}
    del _L0_conv_all

    return {
        "x": x,
        "L0_conv_g1": _L0_conv_in["g1"],
        "L0_conv_b1": _L0_conv_in["b1"],
        "L0_conv_w_qkv": _L0_conv_in["w_qkv"],
        "L0_conv_b_qkv": _L0_conv_in["b_qkv"],
        "L0_conv_rel_pos": _L0_conv_in["rel_pos"],
        "L0_conv_w_proj": _L0_conv_in["w_proj"],
        "L0_conv_b_proj": _L0_conv_in["b_proj"],
        "L0_conv_g2": _L0_conv_in["g2"],
        "L0_conv_b2": _L0_conv_in["b2"],
        "L0_conv_w_mlp1": _L0_conv_in["w_mlp1"],
        "L0_conv_b_mlp1": _L0_conv_in["b_mlp1"],
        "L0_conv_w_mlp2": _L0_conv_in["w_mlp2"],
        "L0_conv_b_mlp2": _L0_conv_in["b_mlp2"],
    }

def reference(x, L0_conv_g1, L0_conv_b1, L0_conv_w_qkv, L0_conv_b_qkv, L0_conv_rel_pos, L0_conv_w_proj, L0_conv_b_proj, L0_conv_g2, L0_conv_b2, L0_conv_w_mlp1, L0_conv_b_mlp1, L0_conv_w_mlp2, L0_conv_b_mlp2):
    import jax
    import jax.numpy as jnp
    def _L0_conv_ref(x, g1, b1, w_qkv, b_qkv, rel_pos, w_proj, b_proj, g2, b2, w_mlp1, b_mlp1, w_mlp2, b_mlp2):
        import jax, jax.numpy as jnp
        import numpy as np
        B, H, W, C = (16, 64, 64, 192)
        HEAD_DIM, N_HEADS, P = (32, 6, 8)
        SHIFT = P // 2
        EPS = 1e-05

        def _layernorm(x, g, b):
            mu = jnp.mean(x, -1, keepdims=True)
            var = jnp.mean((x - mu) ** 2, -1, keepdims=True)
            return (x - mu) * jax.lax.rsqrt(var + EPS) * g + b

        def _rel_bias(rel_pos):
            coords = np.stack(np.meshgrid(np.arange(P), np.arange(P), indexing='ij'), -1).reshape(-1, 2)
            rel = coords[:, None] - coords[None, :] + P - 1
            return rel_pos[:, rel[..., 0], rel[..., 1]]

        def _shift_mask():
            hw, ww = (H // P, W // P)
            m = np.zeros((hw, ww, P, P, P, P), dtype=bool)
            s = P - SHIFT
            m[-1, :, :s, :, s:, :] = True
            m[-1, :, s:, :, :s, :] = True
            m[:, -1, :, :s, :, s:] = True
            m[:, -1, :, s:, :, :s] = True
            return m.reshape(hw * ww, P * P, P * P)
        hw, ww = (H // P, W // P)
        nw, pp = (hw * ww, P * P)
        h = _layernorm(x, g1, b1)
        h = jnp.roll(h, (-SHIFT, -SHIFT), axis=(1, 2))
        h = h.reshape(B, hw, P, ww, P, C).transpose(0, 1, 3, 2, 4, 5).reshape(B, nw, pp, C)
        qkv = (h @ w_qkv + b_qkv).reshape(B, nw, pp, 3, N_HEADS, HEAD_DIM)
        q, k, v = (qkv[..., 0, :, :], qkv[..., 1, :, :], qkv[..., 2, :, :])
        sim = jnp.einsum('bnphd,bnqhd->bhnpq', q, k) * HEAD_DIM ** (-0.5)
        sim = sim + _rel_bias(rel_pos)[None, :, None]
        mask = jnp.asarray(_shift_mask())[None, None]
        sim = jnp.where(mask, -jnp.inf, sim)
        probs = jax.nn.softmax(sim, axis=-1)
        attn = jnp.einsum('bhnpq,bnqhd->bnphd', probs, v).reshape(B, nw, pp, C)
        attn = attn @ w_proj + b_proj
        attn = attn.reshape(B, hw, ww, P, P, C).transpose(0, 1, 3, 2, 4, 5).reshape(B, H, W, C)
        attn = jnp.roll(attn, (SHIFT, SHIFT), axis=(1, 2))
        x = x + attn
        h = _layernorm(x, g2, b2)
        h = jax.nn.gelu(h @ w_mlp1 + b_mlp1, approximate=False)
        x = x + (h @ w_mlp2 + b_mlp2)
        return x

    def _gn(v, G=32, eps=1e-5):
        B_, H_, W_, C_ = v.shape
        g = v.reshape(B_, H_, W_, G, C_ // G)
        m = jnp.mean(g, axis=(1, 2, 4), keepdims=True)
        s = jnp.var(g, axis=(1, 2, 4), keepdims=True)
        return ((g - m) / jnp.sqrt(s + eps)).reshape(v.shape)

    def _ln_c(v, eps=1e-6):
        m = jnp.mean(v, axis=-1, keepdims=True)
        s = jnp.var(v, axis=-1, keepdims=True)
        return (v - m) / jnp.sqrt(s + eps)

    def _ln_t(v, eps=1e-5):
        m = jnp.mean(v, axis=-1, keepdims=True)
        s = jnp.var(v, axis=-1, keepdims=True)
        return (v - m) / jnp.sqrt(s + eps)

    def _to_tokens(v):
        B_, H_, W_, C_ = v.shape
        return v.reshape(B_, H_ * W_, C_)
    def _from_tokens(t, like):
        return t.reshape(like.shape)

    x = _L0_conv_ref(x, L0_conv_g1, L0_conv_b1, L0_conv_w_qkv, L0_conv_b_qkv, L0_conv_rel_pos, L0_conv_w_proj, L0_conv_b_proj, L0_conv_g2, L0_conv_b2, L0_conv_w_mlp1, L0_conv_b_mlp1, L0_conv_w_mlp2, L0_conv_b_mlp2)
    return x


_drawn_inputs = setup_inputs


def setup_inputs(seed=0):
    import zlib

    import numpy as np

    out = dict(_drawn_inputs(seed))
    spreads = {'L0_conv_g1': (1.0, 0.6),
     'L0_conv_b1': (0.0, 0.8),
     'L0_conv_b_qkv': (0.0, 0.3),
     'L0_conv_b_proj': (0.0, 0.1),
     'L0_conv_g2': (1.0, 0.6),
     'L0_conv_b2': (0.0, 0.8),
     'L0_conv_b_mlp1': (0.0, 0.1),
     'L0_conv_b_mlp2': (0.0, 0.1)}
    factors = {'L0_conv_w_qkv': 4.172, 'L0_conv_rel_pos': 8.0}
    for name, (base, spread) in spreads.items():
        noise = np.random.default_rng([zlib.crc32(name.encode()), seed]).standard_normal(out[name].shape)
        drawn = base * np.exp(spread * noise) if base else spread * noise
        out[name] = jnp.asarray(drawn.astype(out[name].dtype))
    for name, factor in factors.items():
        out[name] = (out[name] * factor).astype(out[name].dtype)
    return out
```

```python
from contextlib import ExitStack

import numpy as np

import concourse.bass as bass
from concourse import mybir

F32 = mybir.dt.float32
F32R = mybir.dt.float32r
ALU = mybir.AluOpType
ACT = mybir.ActivationFunctionType
AX_X = mybir.AxisListType.X

P = 128
B, H, W, C = 16, 64, 64, 192
HEADS, HD, WIN = 6, 32, 8
SHIFT = WIN // 2
WT = WIN * WIN
NWIN = W // WIN
T = WIN * W
NT = T // P
G = B * H // WIN
GPI = H // WIN
CB = C - P
HID = 4 * C
NH1 = HID // P
EPS = 1e-5
QSCALE = HD ** -0.5
MASKED = -1e30
HEAD_AT = [0, 4, 1, 5, 2, 3]


def swin_block(nc, x, wqkv, bqkv, ln, rel, mask, wproj, bproj, w1, b1, w2, b2, ident, out):
    with ExitStack() as ctx:
        def sb(name, shape, dt=F32):
            return ctx.enter_context(nc.sbuf_tensor(name, shape, dt))

        def sem(name):
            return ctx.enter_context(nc.semaphore(name))

        scores = ctx.enter_context(nc.psum_tensor("scores", [P, 4, 512], F32))
        ring = ctx.enter_context(nc.psum_tensor("ring", [P, 4, 512], F32))
        (PT0, PT1, PT2, PV0, PV1, PJ0, PJ1, TA1, TB1, QK0, QK1, QK2, V0, V1,
         TA2, TB2, H0, H1, H2, H3, H4, H5, Y0, Y1) = [ring[:, i % 4, :] for i in range(24)]
        qk_bank, v_bank, hid_bank, y_bank = (QK0, QK1, QK2), (V0, V1), (H0, H1, H2, H3, H4, H5), (Y0, Y1)
        pt_bank, pv_bank, pj_bank = (PT0, PT1, PT2), (PV0, PV1), (PJ0, PJ1)

        eye = sb("eye", [P, P])
        raw_qkv = sb("raw_qkv", [P, 2, 3 * C])
        raw_w1 = sb("raw_w1", [P, 2, HID])
        lncol = sb("lncol", [P, 8])
        qkv_hi = sb("qkv_hi", [P, 2, 3 * C], F32R)
        qkv_lo = sb("qkv_lo", [P, 2, 3 * C], F32R)
        w1_hi = sb("w1_hi", [P, 2, HID], F32R)
        w1_lo = sb("w1_lo", [P, 2, HID], F32R)
        w2s = sb("w2s", [P, NH1, C])
        wp = sb("wp", [P, 2, C])
        bqkv_col = sb("bqkv_col", [P, 5])
        bias_qkv = sb("bias_qkv", [P, 5])
        b1_col = sb("b1_col", [P, NH1])
        bias_hid = sb("bias_hid", [P, NH1])
        bproj_all = sb("bproj_all", [P, C])
        b2_all = sb("b2_all", [P, C])
        rel_sb = sb("rel_sb", [P, HEADS, 4 * WT])
        mask_sb = sb("mask_sb", [P, 2, 4 * WT])
        bias_att = sb("bias_att", [P, 2, HEADS, 4 * WT])
        mhalf = sb("mhalf", [P, NT])

        xin = sb("xin", [P, NT, C])
        xres = sb("xres", [P, NT, C])
        stats = sb("stats", [P, 2, NT, 6])
        mv = sb("mv", [P, 2, NT, 2])
        veps = sb("veps", [P, 2, NT])
        rstd = sb("rstd", [P, 2, NT])
        xn = sb("xn", [P, 2, NT, 2 * P])
        hA_hi = sb("hA_hi", [P, T], F32R)
        hA_lo = sb("hA_lo", [P, T], F32R)
        hB = sb("hB", [P, T], F32R)
        mA_hi = sb("mA_hi", [P, T], F32R)
        mA_lo = sb("mA_lo", [P, T], F32R)
        mB = sb("mB", [P, T], F32R)
        qT = sb("qT", [P, 2, T])
        kT = sb("kT", [P, 2, T])
        vt = sb("vt", [P, NT, C])
        prob = sb("prob", [P, HEADS, 4 * WT])
        pmax = sb("pmax", [P, HEADS * 4])
        psum_ = sb("psum_", [P, HEADS * 4])
        prec = sb("prec", [P, HEADS * 4])
        pT = sb("pT", [P, HEADS, 2, P])
        attT = sb("attT", [P, 2, T])
        x2 = sb("x2", [P, NT, C])
        x2b = sb("x2b", [P, NT, C])
        hid = sb("hid", [P, NH1, T])
        yt = sb("yt", [P, NT, C])

        consts_in = sem("consts_in")
        prep_w = sem("prep_w")
        prep_mm = sem("prep_mm")
        prep_bias = sem("prep_bias")
        prep_att = sem("prep_att")
        prep_half = sem("prep_half")
        passed = sem("passed")
        x_in = sem("x_in")
        ln_stats = [sem("ln1_stats"), sem("ln2_stats")]
        ln_mv = [sem("ln1_mv"), sem("ln2_mv")]
        ln_eps = [sem("ln1_eps"), sem("ln2_eps")]
        ln_rstd = [sem("ln1_rstd"), sem("ln2_rstd")]
        ln_norm = [sem("ln1_norm"), sem("ln2_norm")]
        ln_dup = [sem("ln1_dup"), sem("ln2_dup")]
        xres_set = sem("xres_set")
        x2b_set = sem("x2b_set")
        turned = [sem("turned1"), sem("turned2")]
        hi_set = [sem("hi1_set"), sem("hi2_set")]
        lo_set = [sem("lo1_set"), sem("lo2_set")]
        qk_mm = sem("qk_mm")
        qk_set = sem("qk_set")
        v_mm = sem("v_mm")
        v_set = sem("v_set")
        s_mm = sem("s_mm")
        s_biased = sem("s_biased")
        s_max = sem("s_max")
        s_less = sem("s_less")
        p_exp = sem("p_exp")
        p_sum = sem("p_sum")
        p_rec = sem("p_rec")
        p_norm = sem("p_norm")
        pt_mm = sem("pt_mm")
        pt_set = sem("pt_set")
        pv_mm = sem("pv_mm")
        att_set = sem("att_set")
        proj_mm = sem("proj_mm")
        x2_set = sem("x2_set")
        hid_mm = sem("hid_mm")
        hid_set = sem("hid_set")
        y_mm = sem("y_mm")
        y_set = sem("y_set")
        y_out = sem("y_out")

        N_CONST = 14
        half_rows = SHIFT * W
        x_halves = x.rearrange("b (r i) w c -> (b r) (i w) c", i=SHIFT)
        out_halves = out.rearrange("b (r i) w c -> (b r) (i w) c", i=SHIFT)
        tiles_of_half = half_rows // P

        def half_at(g, half):
            at = (g >> 3) * (2 * GPI) + ((2 * (g & 7) + 1 + half) & (2 * GPI - 1))
            return at if isinstance(g, int) else nc.s_assert_within(at, 0, 2 * GPI * B - 1)

        def after(eng, s, value):
            if isinstance(value, int) and value <= 0:
                return
            eng.wait_ge(s, value)

        def wait_alone(eng, s, value):
            eng.wait_ge(s, value)
            if not isinstance(value, int):
                eng.sem_inc(passed, 1)

        def ww_cols(ap):
            rows = ap.rearrange("p (i c) -> p i c", c=W)
            regular = rows[:, :, SHIFT:W - SHIFT].rearrange("p i (w j) -> p w i j", j=WIN)
            ends = rows.rearrange("p i (h j) -> p i h j", j=SHIFT)
            wrapped = ends[:, :, 0:2 * NWIN:2 * NWIN - 1, :]
            return regular, wrapped

        def win_cols(ap):
            wins = ap.rearrange("p (w i j) -> p w i j", w=NWIN, j=WIN)
            regular = wins[:, 0:NWIN - 1]
            wrapped = wins[:, NWIN - 1].rearrange("p i (h j) -> p i h j", j=SHIFT)
            return regular, wrapped

        block = ctx.enter_context(nc.Block())

        @block.sync
        def _(sp):
            def load(g):
                after(sp, xres_set, g)
                for half in range(2):
                    sp.dma_start(
                        xin[:, half * tiles_of_half:(half + 1) * tiles_of_half, :],
                        x_halves[half_at(g, half)].rearrange("(t p) c -> p t c", p=P),
                    ).then_inc(x_in, 16)

            def store(g):
                for half in range(2):
                    at = half_at(g, half)
                    wait_alone(sp, y_set, 2 * g + 1 + half)
                    sp.dma_start(
                        out_halves[at].rearrange("(t p) c -> p t c", p=P),
                        yt[:, half * tiles_of_half:(half + 1) * tiles_of_half, :],
                    ).then_inc(y_out, 16)

            load(0)
            for dst, src in (
                (lncol[:], ln), (raw_qkv[:], wqkv), (bqkv_col[:], bqkv), (eye[:], ident),
                (rel_sb[:], rel), (mask_sb[:], mask), (wp[:], wproj),
                (bproj_all[:], bproj.partition_broadcast(P)), (raw_w1[:], w1), (b1_col[:], b1),
                (w2s[:], w2), (b2_all[:], b2.partition_broadcast(P)),
            ):
                sp.dma_start(dst, src).then_inc(consts_in, 16)
            load(1)
            with sp.Fori(0, G - 2) as g:
                load(g + 2)
                store(g)
            store(G - 2)
            store(G - 1)
            sp.wait_ge(y_out, 32 * G)

        @block.tensor
        def _(pe):
            def mm(dst, lhs, rhs, first=True, last=True):
                return pe.matmul(dst, lhs, rhs, start=first, stop=last)

            def prep():
                pe.wait_ge(consts_in, 12 * 16)
                col = 0
                for m, (a, n, at) in enumerate(((0, P, 0), (P, P, 0), (2 * P, CB, 0), (2 * P + CB, CB, CB),
                                                (2 * C, P, 0), (2 * C + P, CB, 0))):
                    col = m if m < 3 else m - 1
                    dst = PT0[at:at + n, col:col + 1]
                    mm(dst, raw_qkv[:, 0, a:a + n], lncol[:, 2:3], True, False)
                    mm(dst, raw_qkv[0:CB, 1, a:a + n], lncol[0:CB, 3:4], False, True)
                for m in range(NH1):
                    dst = PT1[:, m:m + 1]
                    mm(dst, raw_w1[:, 0, m * P:(m + 1) * P], lncol[:, 6:7], True, False)
                    last = mm(dst, raw_w1[0:CB, 1, m * P:(m + 1) * P], lncol[0:CB, 7:8], False, True)
                last.then_inc(prep_mm, 1)

            def turn(g, n, bank_a, bank_b):
                pe.wait_ge(ln_dup[n], g + 1)
                for part, bank in ((0, bank_a), (1, bank_b)):
                    for t in range(NT):
                        last = pe.transpose(bank[:, t * P:(t + 1) * P],
                                            xn[:, n, t, part * P:(part + 1) * P], eye[:])
                    last.then_inc(turned[n], 1)

            def product(dst, w_hi, w_lo, cols, a_hi, a_lo, b, g, n, wait):
                if wait:
                    pe.wait_ge(hi_set[n], 2 * g + 2)
                mm(dst, w_hi[:, 0, cols], a_hi, True, False)
                mm(dst, w_lo[:, 0, cols], a_hi, False, False)
                if wait:
                    pe.wait_ge(lo_set[n], 2 * g + 1)
                mm(dst, w_hi[:, 0, cols], a_lo, False, False)
                if wait:
                    pe.wait_ge(lo_set[n], 2 * g + 2)
                mm(dst, w_hi[:, 1, cols], b, False, False)
                return mm(dst, w_lo[:, 1, cols], b, False, True)

            def front(g):
                pe.wait_ge(att_set, g) if not isinstance(g, int) or g > 0 else None
                turn(g, 0, TA1, TB1)
                after(pe, x2_set, 2 * g)
                for m in range(3):
                    if m == 2:
                        pe.wait_ge(lo_set[0], 2 * g + 1)
                    product(qk_bank[m], qkv_hi, qkv_lo, slice(m * P, (m + 1) * P),
                            hA_hi[:], hA_lo[:], hB[:], g, 0, m == 0).then_inc(qk_mm, 1)
                cols = slice(2 * C, 3 * C)
                for v in range(2):
                    if v == 1:
                        pe.wait_ge(qk_set, 3 * g + 1)
                    for u in range(2):
                        t = slice((2 * v + u) * P, (2 * v + u + 1) * P)
                        dst = v_bank[v][:, u * C:(u + 1) * C]
                        mm(dst, hA_hi[:, t], qkv_hi[:, 0, cols], True, False)
                        mm(dst, hA_hi[:, t], qkv_lo[:, 0, cols], False, False)
                        mm(dst, hA_lo[:, t], qkv_hi[:, 0, cols], False, False)
                        mm(dst, hB[:, t], qkv_hi[:, 1, cols], False, False)
                        last = mm(dst, hB[:, t], qkv_lo[:, 1, cols], False, True)
                    last.then_inc(v_mm, 1)
                after(pe, s_biased, 2 * g)
                pe.wait_ge(qk_set, 3 * g + 2)
                for heads in ((0, 1, 2, 3), (4, 5)):
                    if heads[0] == 4:
                        pe.wait_ge(qk_set, 3 * g + 3)
                    for tt in range(2):
                        for w in range(2):
                            for tp in range(2):
                                for h in heads:
                                    ww = 4 * tt + 2 * tp + w
                                    r = h % 4
                                    rows = slice(HD * r, HD * (r + 1))
                                    at = (h // 4) * 4 * WT + (2 * tt + w) * WT
                                    last = mm(scores[WT * tp:WT * (tp + 1), r, at:at + WT],
                                              qT[rows, h // 4, ww * WT:(ww + 1) * WT],
                                              kT[rows, h // 4, ww * WT:(ww + 1) * WT])
                    last.then_inc(s_mm, 1)

            def back(g):
                for n, u in enumerate((2, 0, 1)):
                    if n < 2:
                        after(pe, hid_set, 6 * (g - 1) + 5 + n)
                    else:
                        after(pe, y_set, 2 * (g - 1) + 1)
                    pe.wait_ge(p_norm, 2 * g + (1 if n == 0 else 2))
                    for v in range(2):
                        for tt in range(2):
                            last = pe.transpose(
                                pt_bank[n][:, (2 * v + tt) * P:(2 * v + tt + 1) * P],
                                prob[:, 2 * u + v, tt * 2 * WT:(tt + 1) * 2 * WT], eye[:])
                    last.then_inc(pt_mm, 1)
                after(pe, y_set, 2 * g)
                for n, u in enumerate((2, 0, 1)):
                    wait_alone(pe, pt_set, 3 * g + 1 + n)
                    for t in range(NT):
                        for v in range(2):
                            for w in range(2):
                                h = HEAD_AT[2 * u + v]
                                keys = slice(WT * w, WT * (w + 1))
                                at = (h // 4) * 4 * WT + t * WT
                                last = mm(pv_bank[w][HD * (h % 4):HD * (h % 4 + 1), at:at + WT],
                                          vt[keys, t, h * HD:(h + 1) * HD],
                                          pT[keys, 2 * u + v, t // 2, (t % 2) * WT:(t % 2 + 1) * WT])
                last.then_inc(pv_mm, 1)
                pe.wait_ge(att_set, g + 1)
                for n in range(2):
                    for u in range(2):
                        t = slice((2 * n + u) * P, (2 * n + u + 1) * P)
                        dst = pj_bank[n][:, u * C:(u + 1) * C]
                        mm(dst, attT[:, 0, t], wp[:, 0, :], True, False)
                        last = mm(dst, attT[0:CB, 1, t], wp[0:CB, 1, :], False, True)
                    last.then_inc(proj_mm, 1)

            def mlp(g, next_front=True):
                if next_front:
                    pe.wait_ge(qk_set, 3 * g + 6)
                turn(g, 1, TA2, TB2)
                if next_front:
                    pe.wait_ge(v_set, 2 * g + 4)
                for m in range(NH1):
                    if m >= 4:
                        pe.wait_ge(hid_set, 6 * g + m - 3)
                    product(hid_bank[m], w1_hi, w1_lo, slice(m * P, (m + 1) * P),
                            mA_hi[:], mA_lo[:], mB[:], g, 1, m == 0).then_inc(hid_mm, 1)
                for n in range(2):
                    pe.wait_ge(hid_set, 6 * g + 6)
                    for u in range(2):
                        t = slice((2 * n + u) * P, (2 * n + u + 1) * P)
                        dst = y_bank[n][:, u * C:(u + 1) * C]
                        for m in range(NH1):
                            last = mm(dst, hid[:, m, t], w2s[:, m, :], m == 0, m == NH1 - 1)
                    last.then_inc(y_mm, 1)

            prep()
            pe.wait_ge(prep_bias, 1)
            pe.wait_ge(prep_w, 1)
            front(0)
            back(0)
            front(1)
            mlp(0)
            with pe.Fori(1, G - 1) as g:
                back(g)
                front(g + 1)
                mlp(g)
            back(G - 1)
            mlp(G - 1, False)

        @block.scalar
        def _(act):
            def back(g):
                for n, u in enumerate((2, 0, 1)):
                    act.wait_ge(pt_mm, 3 * g + 1 + n)
                    act.copy(pT[:, 2 * u:2 * u + 2].rearrange("p h t q -> p (h t q)"),
                             pt_bank[n][:, :]).then_inc(pt_set, 1)

            def front(g):
                for n, (bank, dst) in enumerate(((TA1, hA_hi), (TB1, hB))):
                    act.wait_ge(turned[0], 2 * g + 1 + n)
                    src_r, src_w = ww_cols(bank)
                    dst_r, dst_w = win_cols(dst[:])
                    act.copy(dst_r, src_r)
                    act.copy(dst_w, src_w).then_inc(hi_set[0], 1)
                for m in range(3):
                    act.wait_ge(qk_mm, 3 * g + 1 + m)
                    if m < 2:
                        act.activation((qT, kT)[m][:, 0, :], qk_bank[m], ACT.Identity,
                                       bias=bias_qkv[:, m:m + 1]).then_inc(qk_set, 1)
                    else:
                        act.activation(qT[0:CB, 1, :], qk_bank[m][0:CB, :], ACT.Identity,
                                       bias=bias_qkv[0:CB, m:m + 1])
                        act.activation(kT[0:CB, 1, :], qk_bank[m][CB:P, :], ACT.Identity,
                                       bias=bias_qkv[CB:P, m:m + 1]).then_inc(qk_set, 1)

            def exps(g):
                for n, hs in enumerate((slice(4, 6), slice(0, 4))):
                    act.wait_ge(s_less, 2 * g + 1 + n)
                    act.activation(prob[:, hs], prob[:, hs], ACT.Exp).then_inc(p_exp, 1)

            def mlp(g):
                for n, (bank, dst) in enumerate(((TA2, mA_hi), (TB2, mB))):
                    act.wait_ge(turned[1], 2 * g + 1 + n)
                    act.copy(dst[:], bank).then_inc(hi_set[1], 1)
                for m in range(NH1):
                    act.wait_ge(hid_mm, 6 * g + 1 + m)
                    act.activation(hid[:, m, :], hid_bank[m], ACT.Gelu,
                                   bias=bias_hid[:, m:m + 1]).then_inc(hid_set, 1)

            act.wait_ge(prep_bias, 1)
            front(0)
            exps(0)
            back(0)
            front(1)
            mlp(0)
            exps(1)
            with act.Fori(1, G - 1) as g:
                back(g)
                front(g + 1)
                mlp(g)
                exps(g + 1)
            back(G - 1)
            mlp(G - 1)

        @block.vector
        def _(dve):
            def prep():
                dve.memset(mhalf[:], -0.5).then_inc(prep_half, 1)
                dve.wait_ge(consts_in, 12 * 16)
                for n in range(2):
                    for a, b, s in ((0, P, QSCALE), (P, 2 * P, 1.0), (2 * P, 2 * P + CB, QSCALE),
                                    (2 * P + CB, 3 * C, 1.0)):
                        dve.tensor_scalar(qkv_hi[:, n, a:b], raw_qkv[:, n, a:b], lncol[:, n:n + 1], s,
                                          ALU.mult, ALU.mult)
                    dve.tensor_scalar(w1_hi[:, n, :], raw_w1[:, n, :], lncol[:, 4 + n:5 + n], None, ALU.mult)
                dve.wait_ge(prep_mm, 1)
                for n in range(2):
                    for a, b, s in ((0, P, QSCALE), (P, 2 * P, 1.0), (2 * P, 2 * P + CB, QSCALE),
                                    (2 * P + CB, 3 * C, 1.0)):
                        dve.tensor_scalar(raw_qkv[:, n, a:b], raw_qkv[:, n, a:b], lncol[:, n:n + 1], s,
                                          ALU.mult, ALU.mult)
                    last = dve.tensor_scalar(raw_w1[:, n, :], raw_w1[:, n, :], lncol[:, 4 + n:5 + n], None,
                                             ALU.mult)
                last.then_inc(prep_w, 1)
                dve.wait_ge(prep_w, 1)
                dve.tensor_tensor(qkv_lo[:], raw_qkv[:], qkv_hi[:], ALU.subtract)
                dve.tensor_tensor(w1_lo[:], raw_w1[:], w1_hi[:], ALU.subtract)
                dve.tensor_tensor(bias_qkv[:, 0:4], PT0[:, 0:4], bqkv_col[:, 0:4], ALU.add)
                dve.tensor_tensor(bias_qkv[0:CB, 4:5], PT0[0:CB, 4:5], bqkv_col[0:CB, 4:5], ALU.add)
                dve.tensor_tensor(bias_hid[:], PT1[:, 0:NH1], b1_col[:], ALU.add).then_inc(prep_w, 1)
                dve.wait_ge(prep_w, 2)
                dve.tensor_scalar(bias_qkv[:, 0:1], bias_qkv[:, 0:1], QSCALE, None, ALU.mult)
                dve.tensor_scalar(bias_qkv[0:CB, 2:3], bias_qkv[0:CB, 2:3], QSCALE, None,
                                  ALU.mult).then_inc(prep_bias, 1)
                for kind in range(2):
                    for h in range(HEADS):
                        last = dve.tensor_tensor(bias_att[:, kind, h, :], rel_sb[:, h, :],
                                                 mask_sb[:, kind, :], ALU.add)
                last.then_inc(prep_att, 1)

            def moments(g, n, src):
                for t in range(NT):
                    last = dve.bn_stats(stats[:, n, t, :], src[:, t, :])
                last.then_inc(ln_stats[n], 1)
                wait_alone(dve, ln_stats[n], g + 1)
                for t in range(NT):
                    last = dve.bn_aggr(mv[:, n, t, :], stats[:, n, t, :])
                last.then_inc(ln_mv[n], 1)

            def ln1(g):
                dve.wait_ge(x_in, 32 * g + 32)
                moments(g, 0, xin)

            def back(g):
                dve.wait_ge(pv_mm, g + 1)
                for part, rows in ((0, P), (1, CB)):
                    plain_r, plain_w = ww_cols(attT[0:rows, part, :])
                    for w in range(2):
                        src = pv_bank[w][0:rows, part * 4 * WT:(part + 1) * 4 * WT].rearrange(
                            "p (t i j) -> p t i j", t=NT, j=WIN)
                        bias = bias_qkv[0:rows, 3 + part:4 + part]
                        n = NT - w
                        last = dve.tensor_scalar(plain_r[:, w:NWIN - 1:2], src[:, 0:n], bias, None, ALU.add)
                        if w == 1:
                            last = dve.tensor_scalar(
                                plain_w, src[:, NT - 1].rearrange("p i (h j) -> p i h j", j=SHIFT),
                                bias, None, ALU.add)
                last.then_inc(att_set, 1)
                after(dve, x2b_set, g)
                dve.wait_ge(xres_set, g + 1)
                for n in range(2):
                    dve.wait_ge(proj_mm, 2 * g + 1 + n)
                    dve.tensor_tensor(x2[:, 2 * n:2 * n + 2, :], xres[:, 2 * n:2 * n + 2, :],
                                      pj_bank[n][:, 0:2 * C].rearrange("p (t c) -> p t c", c=C),
                                      ALU.add).then_inc(x2_set, 1)
                dve.wait_ge(x2_set, 2 * g + 2)
                moments(g, 1, x2)

            def front(g):
                dve.wait_ge(hi_set[0], 2 * g + 1)
                for (d, s, h) in zip(win_cols(hA_lo[:]), ww_cols(TA1), win_cols(hA_hi[:])):
                    last = dve.tensor_tensor(d, s, h, ALU.subtract)
                last.then_inc(lo_set[0], 1)
                dve.wait_ge(hi_set[0], 2 * g + 2)
                for (d, s, h) in zip(win_cols(hB[CB:P, :]), ww_cols(TB1[CB:P, :]), win_cols(hB[CB:P, :])):
                    last = dve.tensor_tensor(d, s, h, ALU.subtract)
                last.then_inc(lo_set[0], 1)
                for n in range(2):
                    dve.wait_ge(v_mm, 2 * g + 1 + n)
                    dve.tensor_copy(vt[:, 2 * n:2 * n + 2, :].rearrange("p t c -> p (t c)"),
                                    v_bank[n][:, 0:2 * C]).then_inc(v_set, 1)

            def softmax(g):
                last_row = ((g & 7) + 1) >> 3
                for n, (src, hs) in enumerate((
                    (scores[:, 2:4, 0:4 * WT], slice(4, 6)),
                    (scores[:, 0:2, :].rearrange("p b (s k) -> p (b s) k", s=2), slice(0, 4)),
                )):
                    dve.wait_ge(s_mm, 2 * g + 1 + n)
                    dve.tensor_tensor(prob[:, hs, :], src, bias_att[:, last_row, hs, :],
                                      ALU.add).then_inc(s_biased, 1)
                    rows = slice(hs.start * 4, hs.stop * 4)
                    p3 = prob[:, hs, :].rearrange("p h (w k) -> p (h w) k", k=WT)
                    dve.wait_ge(s_biased, 2 * g + 1 + n)
                    dve.tensor_reduce(pmax[:, rows], p3, AX_X, ALU.max).then_inc(s_max, 1)
                    dve.wait_ge(s_max, 2 * g + 1 + n)
                    dve.tensor_tensor(p3, p3, pmax[:, rows].unsqueeze(2).broadcast_to([P, rows.stop - rows.start, WT]),
                                      ALU.subtract).then_inc(s_less, 1)

            def sums(g):
                for n, hs in enumerate((slice(4, 6), slice(0, 4))):
                    rows = slice(hs.start * 4, hs.stop * 4)
                    p3 = prob[:, hs, :].rearrange("p h (w k) -> p (h w) k", k=WT)
                    dve.wait_ge(p_exp, 2 * g + 1 + n)
                    dve.tensor_reduce(psum_[:, rows], p3, AX_X, ALU.add).then_inc(p_sum, 1)
                    dve.wait_ge(p_sum, 2 * g + 1 + n)
                    dve.reciprocal(prec[:, rows], psum_[:, rows]).then_inc(p_rec, 1)

            def mlp_lo(g):
                dve.wait_ge(hi_set[1], 2 * g + 1)
                dve.tensor_tensor(mA_lo[:], TA2, mA_hi[:], ALU.subtract).then_inc(lo_set[1], 1)
                dve.wait_ge(hi_set[1], 2 * g + 2)
                dve.tensor_tensor(mB[CB:P, :], TB2[CB:P, :], mB[CB:P, :], ALU.subtract).then_inc(lo_set[1], 1)

            def result(g):
                dve.wait_ge(x2b_set, g + 1)
                after(dve, y_out, 32 * g)
                for n in range(2):
                    dve.wait_ge(y_mm, 2 * g + 1 + n)
                    dve.tensor_tensor(yt[:, 2 * n:2 * n + 2, :], x2b[:, 2 * n:2 * n + 2, :],
                                      y_bank[n][:, 0:2 * C].rearrange("p (t c) -> p t c", c=C),
                                      ALU.add).then_inc(y_set, 1)

            prep()
            ln1(0)
            front(0)
            dve.wait_ge(prep_att, 1)
            softmax(0)
            sums(0)
            ln1(1)
            back(0)
            front(1)
            mlp_lo(0)
            softmax(1)
            sums(1)
            result(0)
            with dve.Fori(1, G - 1) as g:
                ln1(g + 1)
                back(g)
                front(g + 1)
                mlp_lo(g)
                softmax(g + 1)
                sums(g + 1)
                result(g)
            back(G - 1)
            mlp_lo(G - 1)
            result(G - 1)

        @block.gpsimd
        def _(pool):
            def normalise(g, n, src):
                wait_alone(pool, ln_mv[n], g + 1)
                pool.tensor_scalar(veps[:, n, :], mv[:, n, :, 1], EPS, None, ALU.add).then_inc(ln_eps[n], 1)
                pool.wait_ge(ln_eps[n], g + 1)
                pool.tensor_tensor(rstd[:, n, :], veps[:, n, :], mhalf[:], ALU.pow).then_inc(ln_rstd[n], 1)
                after(pool, turned[n], 2 * g)
                wait_alone(pool, ln_rstd[n], g + 1)
                for t in range(NT):
                    last = pool.tensor_scalar(xn[:, n, t, 0:C], src[:, t, :], mv[:, n, t, 0:1],
                                              rstd[:, n, t:t + 1], ALU.subtract, ALU.mult)
                last.then_inc(ln_norm[n], 1)
                wait_alone(pool, ln_norm[n], g + 1)
                pool.tensor_copy(xn[:, n, :, C:2 * P], xn[:, n, :, P:C]).then_inc(ln_dup[n], 1)

            def keep_x(g):
                after(pool, x2_set, 2 * g)
                pool.tensor_tensor(xres[:], xin[:], bproj_all[:].unsqueeze(1).broadcast_to([P, NT, C]),
                                   ALU.add).then_inc(xres_set, 1)

            def keep_x2(g):
                after(pool, y_set, 2 * g)
                pool.tensor_tensor(x2b[:], x2[:], b2_all[:].unsqueeze(1).broadcast_to([P, NT, C]),
                                   ALU.add).then_inc(x2b_set, 1)

            def probs(g):
                for n, hs in enumerate((slice(4, 6), slice(0, 4))):
                    rows = slice(hs.start * 4, hs.stop * 4)
                    p3 = prob[:, hs, :].rearrange("p h (w k) -> p (h w) k", k=WT)
                    pool.wait_ge(p_rec, 2 * g + 1 + n)
                    pool.tensor_tensor(p3, p3, prec[:, rows].unsqueeze(2).broadcast_to([P, rows.stop - rows.start, WT]),
                                       ALU.mult).then_inc(p_norm, 1)

            pool.wait_ge(prep_half, 1)
            normalise(0, 0, xin)
            pool.wait_ge(consts_in, 12 * 16)
            keep_x(0)
            probs(0)
            normalise(1, 0, xin)
            normalise(0, 1, x2)
            keep_x2(0)
            keep_x(1)
            probs(1)
            with pool.Fori(1, G - 1) as g:
                normalise(g + 1, 0, xin)
                normalise(g, 1, x2)
                keep_x2(g)
                keep_x(g + 1)
                probs(g + 1)
            normalise(G - 1, 1, x2)
            keep_x2(G - 1)


def _token(win_kind):
    i, j = np.meshgrid(np.arange(WIN), np.arange(WIN), indexing="ij")
    if win_kind == "wrapped":
        j = (j + SHIFT) % WIN
    return i.ravel(), j.ravel()


def _places():
    iq = np.zeros((P, 4 * WT), np.int64)
    jq, ik, jk, wrap = iq.copy(), iq.copy(), iq.copy(), np.zeros((P, 4 * WT), bool)
    for tp in range(2):
        for tt in range(2):
            for w in range(2):
                last = 4 * tt + 2 * tp + w == NWIN - 1
                i, j = _token("wrapped" if last else "regular")
                rows, cols = slice(WT * tp, WT * (tp + 1)), slice((2 * tt + w) * WT, (2 * tt + w + 1) * WT)
                iq[rows, cols], jq[rows, cols] = i[:, None], j[:, None]
                ik[rows, cols], jk[rows, cols] = i[None, :], j[None, :]
                wrap[rows, cols] = last
    return iq, jq, ik, jk, wrap


def _lay_out(inputs):
    a = {k: np.asarray(v) for k, v in inputs.items()}
    f = np.float32
    p = "L0_conv_"

    def two_parts(w):
        return np.ascontiguousarray(np.stack([w[:P], np.concatenate([w[P:], w[P:]])], 1))

    def two_cols(v):
        return np.stack([v[:P], np.concatenate([v[P:], v[P:]])], 1)

    order = np.concatenate([np.arange(0, P), np.arange(C, C + P), np.arange(P, C), np.arange(C + P, 2 * C),
                            np.arange(2 * C, 3 * C)])
    bq = a[p + "b_qkv"][order]
    zeros = np.zeros(CB, f)
    bqkv = np.stack([bq[0:P], bq[P:2 * P], bq[2 * P:3 * P], bq[2 * C:2 * C + P],
                     np.concatenate([bq[2 * C + P:], zeros])], 1)
    ln = np.concatenate([two_cols(a[p + n]) for n in ("g1", "b1", "g2", "b2")], 1)
    iq, jq, ik, jk, wrap = _places()
    rel = a[p + "rel_pos"][HEAD_AT][:, iq - ik + WIN - 1, jq - jk + WIN - 1].transpose(1, 0, 2)
    across_cols = wrap & ((jq < SHIFT) != (jk < SHIFT))
    across_rows = (iq < SHIFT) != (ik < SHIFT)
    mask = np.stack([across_cols, across_cols | across_rows], 1).astype(f) * f(MASKED)
    c = np.ascontiguousarray
    return {
        "x": c(a["x"]), "wqkv": two_parts(a[p + "w_qkv"][:, order]), "bqkv": c(bqkv), "ln": c(ln),
        "rel": c(rel), "mask": c(mask), "wproj": two_parts(a[p + "w_proj"]), "bproj": c(a[p + "b_proj"]),
        "w1": two_parts(a[p + "w_mlp1"]), "b1": c(a[p + "b_mlp1"].reshape(NH1, P).T),
        "w2": c(a[p + "w_mlp2"].reshape(NH1, P, C).transpose(1, 0, 2)), "b2": c(a[p + "b_mlp2"]),
        "ident": np.eye(P, dtype=f),
    }


def kernel(**inputs):
    import concourse.bacc as bacc
    from concourse.bass_utils import run_bass_kernel_spmd

    arrays = _lay_out(inputs)
    nc = bacc.Bacc("TRN2", target_bir_lowering=False, num_devices=1)
    args = {k: nc.dram_tensor(f"in_{k}", v.shape, F32, kind="ExternalInput").ap() for k, v in arrays.items()}
    out = nc.dram_tensor("out", (B, H, W, C), F32, kind="ExternalOutput").ap()
    swin_block(nc, out=out, **args)
    r = run_bass_kernel_spmd(nc, [{f"in_{k}": v for k, v in arrays.items()}], core_ids=[0])
    return r.results[0]["out"]
```

```python
from contextlib import ExitStack

import numpy as np

import concourse.bass as bass
from concourse import mybir

F32 = mybir.dt.float32
F32R = mybir.dt.float32r
ALU = mybir.AluOpType
ACT = mybir.ActivationFunctionType
AX_X = mybir.AxisListType.X

P = 128
B, H, W, C = 16, 64, 64, 192
HEADS, HD, WIN = 6, 32, 8
SHIFT = WIN // 2
WT = WIN * WIN
NWIN = W // WIN
T = WIN * W
NT = T // P
G = B * H // WIN
GPI = H // WIN
CB = C - P
HID = 4 * C
NH1 = HID // P
EPS = 1e-5
QSCALE = HD ** -0.5
MASKED = -1e30
HEAD_AT = [0, 4, 1, 5, 2, 3]


def swin_block(nc, x, wqkv, bqkv, ln, rel, mask, wproj, bproj, w1, b1, w2, b2, ident, out):
    with ExitStack() as ctx:
        def sb(name, shape, dt=F32):
            return ctx.enter_context(nc.sbuf_tensor(name, shape, dt))

        def sem(name):
            return ctx.enter_context(nc.semaphore(name))

        scores = ctx.enter_context(nc.psum_tensor("scores", [P, 4, 512], F32))
        ring = ctx.enter_context(nc.psum_tensor("ring", [P, 4, 512], F32))
        PT0, PT1, PT2, Y1 = [scores[:, i, :] for i in range(4)]
        (PV0, PV1, TA1, TB1, PJ0, PJ1, QK0, QK1, QK2, V0, V1,
         TA2, TB2, H0, H1, H2, H3, H4, H5, Y0) = [ring[:, i % 4, :] for i in range(20)]
        qk_bank, v_bank, hid_bank, y_bank = (QK0, QK1, QK2), (V0, V1), (H0, H1, H2, H3, H4, H5), (Y0, Y1)
        pt_bank, pj_bank = (PT0, PT1, PT2), (PJ0, PJ1)

        eye = sb("eye", [P, P])
        raw_qkv = sb("raw_qkv", [P, 2, 3 * C])
        raw_w1 = sb("raw_w1", [P, 2, HID])
        lncol = sb("lncol", [P, 8])
        qkv_hi = sb("qkv_hi", [P, 2, 3 * C], F32R)
        qkv_lo = sb("qkv_lo", [P, 2, 3 * C], F32R)
        w1_hi = sb("w1_hi", [P, 2, HID], F32R)
        w1_lo = sb("w1_lo", [P, 2, HID], F32R)
        w2s = sb("w2s", [P, NH1, C])
        wp = sb("wp", [P, 2, C])
        bqkv_col = sb("bqkv_col", [P, 5])
        bias_qkv = sb("bias_qkv", [P, 5])
        b1_col = sb("b1_col", [P, NH1])
        bias_hid = sb("bias_hid", [P, NH1])
        bproj_all = sb("bproj_all", [P, C])
        b2_all = sb("b2_all", [P, C])
        rel_sb = sb("rel_sb", [P, HEADS, 4 * WT])
        mask_sb = sb("mask_sb", [P, 2, 4 * WT])
        bias_att = sb("bias_att", [P, 2, HEADS, 4 * WT])
        mhalf = sb("mhalf", [P, NT])

        xin = sb("xin", [P, NT, C])
        xres = sb("xres", [P, NT, C])
        stats = sb("stats", [P, 2, NT, 6])
        mv = sb("mv", [P, 2, NT, 2])
        veps = sb("veps", [P, 2, NT])
        rstd = sb("rstd", [P, 2, NT])
        xn = sb("xn", [P, 2, NT, 2 * P])
        hA_hi = sb("hA_hi", [P, T], F32R)
        hA_lo = sb("hA_lo", [P, T], F32R)
        hB = sb("hB", [P, T], F32R)
        mA_hi = sb("mA_hi", [P, T], F32R)
        mA_lo = sb("mA_lo", [P, T], F32R)
        mB = sb("mB", [P, T], F32R)
        qT = sb("qT", [P, 2, T])
        kT = sb("kT", [P, 2, T])
        vt = sb("vt", [P, NT, C])
        prob = sb("prob", [P, HEADS, 4 * WT])
        pmax = sb("pmax", [P, HEADS * 4])
        psum_ = sb("psum_", [P, HEADS * 4])
        prec = sb("prec", [P, HEADS * 4])
        pT = sb("pT", [P, HEADS, NT, P])
        attT = sb("attT", [P, 2, T])
        x2 = sb("x2", [P, NT, C])
        x2b = sb("x2b", [P, NT, C])
        hid = sb("hid", [P, NH1, T])
        yt = sb("yt", [P, NT, C])

        consts_in = sem("consts_in")
        prep_w = sem("prep_w")
        prep_mm = sem("prep_mm")
        prep_bias = sem("prep_bias")
        prep_att = sem("prep_att")
        prep_half = sem("prep_half")
        passed = sem("passed")
        x_in = sem("x_in")
        ln_stats = [sem("ln1_stats"), sem("ln2_stats")]
        ln_mv = [sem("ln1_mv"), sem("ln2_mv")]
        ln_eps = [sem("ln1_eps"), sem("ln2_eps")]
        ln_rstd = [sem("ln1_rstd"), sem("ln2_rstd")]
        ln_norm = [sem("ln1_norm"), sem("ln2_norm")]
        ln_dup = [sem("ln1_dup"), sem("ln2_dup")]
        xres_set = sem("xres_set")
        x2b_set = sem("x2b_set")
        turned = [sem("turned1"), sem("turned2")]
        hi_set = [sem("hi1_set"), sem("hi2_set")]
        lo_set = [sem("lo1_set"), sem("lo2_set")]
        qk_mm = sem("qk_mm")
        qk_set = sem("qk_set")
        v_mm = sem("v_mm")
        v_set = sem("v_set")
        s_mm = sem("s_mm")
        s_biased = sem("s_biased")
        s_max = sem("s_max")
        s_less = sem("s_less")
        p_exp = sem("p_exp")
        p_sum = sem("p_sum")
        p_rec = sem("p_rec")
        p_norm = sem("p_norm")
        pt_mm = sem("pt_mm")
        pt_set = [sem("pt_set0"), sem("pt_set1")]
        pt_zero = sem("pt_zero")
        pv_mm = sem("pv_mm")
        att_set = [sem("attA_set"), sem("attB_set")]
        proj_mm = sem("proj_mm")
        x2_set = sem("x2_set")
        hid_mm = sem("hid_mm")
        hid_set = sem("hid_set")
        y_mm = sem("y_mm")
        y_set = sem("y_set")
        y_out = sem("y_out")

        N_CONST = 14
        half_rows = SHIFT * W
        x_halves = x.rearrange("b (r i) w c -> (b r) (i w) c", i=SHIFT)
        out_halves = out.rearrange("b (r i) w c -> (b r) (i w) c", i=SHIFT)
        tiles_of_half = half_rows // P

        def half_at(g, half):
            at = (g >> 3) * (2 * GPI) + ((2 * (g & 7) + 1 + half) & (2 * GPI - 1))
            return at if isinstance(g, int) else nc.s_assert_within(at, 0, 2 * GPI * B - 1)

        def after(eng, s, value):
            if isinstance(value, int) and value <= 0:
                return
            eng.wait_ge(s, value)

        def wait_alone(eng, s, value):
            eng.wait_ge(s, value)
            if not isinstance(value, int):
                eng.sem_inc(passed, 1)

        def ww_cols(ap):
            rows = ap.rearrange("p (i c) -> p i c", c=W)
            regular = rows[:, :, SHIFT:W - SHIFT].rearrange("p i (w j) -> p w i j", j=WIN)
            ends = rows.rearrange("p i (h j) -> p i h j", j=SHIFT)
            wrapped = ends[:, :, 0:2 * NWIN:2 * NWIN - 1, :]
            return regular, wrapped

        def win_cols(ap):
            wins = ap.rearrange("p (w i j) -> p w i j", w=NWIN, j=WIN)
            regular = wins[:, 0:NWIN - 1]
            wrapped = wins[:, NWIN - 1].rearrange("p i (h j) -> p i h j", j=SHIFT)
            return regular, wrapped

        block = ctx.enter_context(nc.Block())

        @block.sync
        def _(sp):
            def load(g):
                after(sp, ln_norm[0], g)
                after(sp, xres_set, g)
                for half in range(2):
                    sp.dma_start(
                        xin[:, half * tiles_of_half:(half + 1) * tiles_of_half, :],
                        x_halves[half_at(g, half)].rearrange("(t p) c -> p t c", p=P),
                    ).then_inc(x_in, 16)

            def store(g):
                for half in range(2):
                    at = half_at(g, half)
                    wait_alone(sp, y_set, 2 * g + 1 + half)
                    sp.dma_start(
                        out_halves[at].rearrange("(t p) c -> p t c", p=P),
                        yt[:, half * tiles_of_half:(half + 1) * tiles_of_half, :],
                    ).then_inc(y_out, 16)

            load(0)
            for dst, src in (
                (lncol[:], ln), (raw_qkv[:], wqkv), (bqkv_col[:], bqkv), (eye[:], ident),
                (rel_sb[:], rel), (mask_sb[:], mask), (wp[:], wproj),
                (bproj_all[:], bproj.partition_broadcast(P)), (raw_w1[:], w1), (b1_col[:], b1),
                (w2s[:], w2), (b2_all[:], b2.partition_broadcast(P)),
            ):
                sp.dma_start(dst, src).then_inc(consts_in, 16)
            load(1)
            with sp.Fori(0, G - 2) as g:
                load(g + 2)
                store(g)
            store(G - 2)
            store(G - 1)
            sp.wait_ge(y_out, 32 * G)

        @block.tensor
        def _(pe):
            def mm(dst, lhs, rhs, first=True, last=True):
                return pe.matmul(dst, lhs, rhs, start=first, stop=last)

            def prep():
                pe.wait_ge(consts_in, 12 * 16)
                col = 0
                for m, (a, n, at) in enumerate(((0, P, 0), (P, P, 0), (2 * P, CB, 0), (2 * P + CB, CB, CB),
                                                (2 * C, P, 0), (2 * C + P, CB, 0))):
                    col = m if m < 3 else m - 1
                    dst = PT0[at:at + n, col:col + 1]
                    mm(dst, raw_qkv[:, 0, a:a + n], lncol[:, 2:3], True, False)
                    mm(dst, raw_qkv[0:CB, 1, a:a + n], lncol[0:CB, 3:4], False, True)
                for m in range(NH1):
                    dst = PT1[:, m:m + 1]
                    mm(dst, raw_w1[:, 0, m * P:(m + 1) * P], lncol[:, 6:7], True, False)
                    last = mm(dst, raw_w1[0:CB, 1, m * P:(m + 1) * P], lncol[0:CB, 7:8], False, True)
                last.then_inc(prep_mm, 1)

            def turn(g, n, bank_a, bank_b):
                pe.wait_ge(ln_dup[n], g + 1)
                for part, bank in ((0, bank_a), (1, bank_b)):
                    for t in range(NT):
                        last = pe.transpose(bank[:, t * P:(t + 1) * P],
                                            xn[:, n, t, part * P:(part + 1) * P], eye[:])
                    last.then_inc(turned[n], 1)

            def product(dst, w_hi, w_lo, m, a_hi, a_lo, b):
                cols = slice(m * P, (m + 1) * P)
                mm(dst, w_hi[:, 0, cols], a_hi, True, False)
                mm(dst, w_lo[:, 0, cols], a_hi, False, False)
                mm(dst, w_hi[:, 0, cols], a_lo, False, False)
                mm(dst, w_hi[:, 1, cols], b, False, False)
                return mm(dst, w_lo[:, 1, cols], b, False, True)

            def turn1(g):
                after(pe, y_set, 2 * g - 3)
                turn(g, 0, TA1, TB1)

            def v_tile(t):
                cols, at = slice(2 * C, 3 * C), slice(t * P, (t + 1) * P)
                dst = v_bank[t // 2][:, (t % 2) * C:(t % 2 + 1) * C]
                mm(dst, hA_hi[:, at], qkv_hi[:, 0, cols], True, False)
                mm(dst, hA_hi[:, at], qkv_lo[:, 0, cols], False, False)
                mm(dst, hA_lo[:, at], qkv_hi[:, 0, cols], False, False)
                mm(dst, hB[:, at], qkv_hi[:, 1, cols], False, False)
                return mm(dst, hB[:, at], qkv_lo[:, 1, cols], False, True)

            def score_part(heads, tt, w):
                for tp in range(2):
                    for h in heads:
                        ww = 4 * tt + 2 * tp + w
                        r = h % 4
                        rows = slice(HD * r, HD * (r + 1))
                        at = (h // 4) * 4 * WT + (2 * tt + w) * WT
                        last = mm(scores[WT * tp:WT * (tp + 1), r, at:at + WT],
                                  qT[rows, h // 4, ww * WT:(ww + 1) * WT],
                                  kT[rows, h // 4, ww * WT:(ww + 1) * WT])
                return last

            def front(g):
                pe.wait_ge(hi_set[0], 2 * g + 2)
                pe.wait_ge(lo_set[0], 2 * g + 2)
                for m in range(3):
                    if m == 2:
                        after(pe, x2_set, 2 * g - 1)
                    product(qk_bank[m], qkv_hi, qkv_lo, m, hA_hi[:], hA_lo[:], hB[:]).then_inc(qk_mm, 1)
                after(pe, x2_set, 2 * g)
                after(pe, s_biased, 2 * g)
                after(pe, y_set, 2 * g - 2)
                for t in range(NT):
                    if t == 2:
                        pe.wait_ge(qk_set, 3 * g + 1)
                    last = v_tile(t)
                    if t % 2:
                        last.then_inc(v_mm, 1)
                    if t == 0:
                        pe.wait_ge(qk_set, 3 * g + 2)
                    last = score_part((0, 1, 2, 3), t // 2, t % 2)
                last.then_inc(s_mm, 1)

            def turn2(g, woven):
                if woven:
                    pe.wait_ge(qk_set, 3 * g + 6)
                turn(g, 1, TA2, TB2)

            def front_end(g):
                pe.wait_ge(qk_set, 3 * g + 3)
                for t in range(NT):
                    last = score_part((4, 5), t // 2, t % 2)
                last.then_inc(s_mm, 1)

            def turn_probs(g, n):
                u = (2, 0, 1)[n]
                pe.wait_ge(p_norm, 2 * g + (1 if n == 0 else 2))
                for v in range(2):
                    for tt in range(2):
                        last = pe.transpose(
                            pt_bank[n][:, (2 * v + tt) * P:(2 * v + tt + 1) * P],
                            prob[:, 2 * u + v, tt * 2 * WT:(tt + 1) * 2 * WT], eye[:])
                last.then_inc(pt_mm, 1)

            def back(g):
                for n, u in enumerate((2, 0, 1)):
                    pe.wait_ge(pt_set[0], 3 * g + 1 + n)
                    wait_alone(pe, pt_set[1], 3 * g + 1 + n)
                    for t in range(NT):
                        for v in range(2):
                            h = HEAD_AT[2 * u + v]
                            last = mm((PV0, PV1)[h // 4][HD * (h % 4):HD * (h % 4 + 1), t * P:(t + 1) * P],
                                      vt[:, t, h * HD:(h + 1) * HD], pT[:, 2 * u + v, t, :])
                last.then_inc(pv_mm, 1)

            def project(g):
                for n in range(2):
                    for u in range(2):
                        t = slice((2 * n + u) * P, (2 * n + u + 1) * P)
                        dst = pj_bank[n][:, u * C:(u + 1) * C]
                        pe.wait_ge(att_set[0], g + 1)
                        mm(dst, attT[:, 0, t], wp[:, 0, :], True, False)
                        pe.wait_ge(att_set[1], g + 1)
                        last = mm(dst, attT[0:CB, 1, t], wp[0:CB, 1, :], False, True)
                    last.then_inc(proj_mm, 1)

            def mlp(g, woven):
                if woven:
                    pe.wait_ge(v_set, 2 * g + 4)
                pe.wait_ge(hi_set[1], 2 * g + 1)
                for m in range(2):
                    cols = slice(m * P, (m + 1) * P)
                    mm(hid_bank[m], w1_hi[:, 0, cols], mA_hi[:], True, False)
                    mm(hid_bank[m], w1_lo[:, 0, cols], mA_hi[:], False, False)
                for m in range(2):
                    cols = slice(m * P, (m + 1) * P)
                    pe.wait_ge(lo_set[1], 2 * g + 1)
                    mm(hid_bank[m], w1_hi[:, 0, cols], mA_lo[:], False, False)
                    pe.wait_ge(lo_set[1], 2 * g + 2)
                    mm(hid_bank[m], w1_hi[:, 1, cols], mB[:], False, False)
                    mm(hid_bank[m], w1_lo[:, 1, cols], mB[:], False, True).then_inc(hid_mm, 1)
                for m in range(2, NH1):
                    if m >= 4:
                        pe.wait_ge(hid_set, 6 * g + m - 3)
                    product(hid_bank[m], w1_hi, w1_lo, m, mA_hi[:], mA_lo[:], mB[:]).then_inc(hid_mm, 1)
                if woven:
                    pe.wait_ge(s_biased, 2 * g + 3)
                for t in range(NT):
                    if woven and t == NT - 1:
                        turn_probs(g + 1, 0)
                    dst = y_bank[t // 2][:, (t % 2) * C:(t % 2 + 1) * C]
                    for m in range(NH1):
                        if t == 0:
                            pe.wait_ge(hid_set, 6 * g + max(m + 1, 3))
                        last = mm(dst, hid[:, m, t * P:(t + 1) * P], w2s[:, m, :], m == 0, m == NH1 - 1)
                    if t % 2:
                        last.then_inc(y_mm, 1)
                if woven:
                    turn_probs(g + 1, 1)
                    turn_probs(g + 1, 2)

            prep()
            pe.wait_ge(prep_bias, 1)
            pe.wait_ge(prep_w, 1)
            turn1(0)
            front(0)
            front_end(0)
            for n in range(3):
                turn_probs(0, n)
            back(0)
            turn1(1)
            project(0)
            front(1)
            turn2(0, True)
            front_end(1)
            mlp(0, True)
            with pe.Fori(1, G - 1) as g:
                back(g)
                turn1(g + 1)
                project(g)
                front(g + 1)
                turn2(g, True)
                front_end(g + 1)
                mlp(g, True)
            back(G - 1)
            project(G - 1)
            turn2(G - 1, False)
            mlp(G - 1, False)

        @block.scalar
        def _(act):
            def back(g):
                for n, u in enumerate((2, 0, 1)):
                    act.wait_ge(pt_mm, 3 * g + 1 + n)
                    act.copy(pT[0:WT, 2 * u:2 * u + 2, :, 0:WT].rearrange("p h t q -> p (h t) q"),
                             pt_bank[n][0:WT, :].rearrange("p (x q) -> p x q", q=WT)).then_inc(pt_set[0], 1)
                act.wait_ge(pv_mm, g + 1)
                for dst, src in zip(ww_cols(attT[0:CB, 1, :]), win_cols(PV1[0:CB, :])):
                    last = act.activation(dst, src, ACT.Identity, bias=bias_qkv[0:CB, 4:5])
                last.then_inc(att_set[1], 1)

            def front(g):
                for n, (bank, dst) in enumerate(((TA1, hA_hi), (TB1, hB))):
                    act.wait_ge(turned[0], 2 * g + 1 + n)
                    src_r, src_w = ww_cols(bank)
                    dst_r, dst_w = win_cols(dst[:])
                    act.copy(dst_r, src_r)
                    act.copy(dst_w, src_w).then_inc(hi_set[0], 1)
                for m in range(3):
                    act.wait_ge(qk_mm, 3 * g + 1 + m)
                    if m < 2:
                        act.activation((qT, kT)[m][:, 0, :], qk_bank[m], ACT.Identity,
                                       bias=bias_qkv[:, m:m + 1]).then_inc(qk_set, 1)
                    else:
                        act.activation(qT[0:CB, 1, :], qk_bank[m][0:CB, :], ACT.Identity,
                                       bias=bias_qkv[0:CB, m:m + 1])
                        act.activation(kT[0:CB, 1, :], qk_bank[m][CB:P, :], ACT.Identity,
                                       bias=bias_qkv[CB:P, m:m + 1]).then_inc(qk_set, 1)

            def exps(g):
                for n, hs in enumerate((slice(4, 6), slice(0, 4))):
                    act.wait_ge(s_less, 2 * g + 1 + n)
                    act.activation(prob[:, hs], prob[:, hs], ACT.Exp).then_inc(p_exp, 1)

            def mlp(g):
                for n, (bank, dst) in enumerate(((TA2, mA_hi), (TB2, mB))):
                    act.wait_ge(turned[1], 2 * g + 1 + n)
                    act.copy(dst[:], bank).then_inc(hi_set[1], 1)
                for m in range(NH1):
                    act.wait_ge(hid_mm, 6 * g + 1 + m)
                    act.activation(hid[:, m, :], hid_bank[m], ACT.Gelu,
                                   bias=bias_hid[:, m:m + 1]).then_inc(hid_set, 1)

            act.wait_ge(prep_bias, 1)
            act.wait_ge(pt_zero, 1)
            front(0)
            exps(0)
            back(0)
            front(1)
            mlp(0)
            exps(1)
            with act.Fori(1, G - 1) as g:
                back(g)
                front(g + 1)
                mlp(g)
                exps(g + 1)
            back(G - 1)
            mlp(G - 1)

        @block.vector
        def _(dve):
            def prep():
                dve.memset(mhalf[:], -0.5).then_inc(prep_half, 1)
                dve.memset(pT[:].bitcast(mybir.dt.uint32), 0).then_inc(pt_zero, 1)
                dve.wait_ge(pt_zero, 1)
                dve.wait_ge(consts_in, 12 * 16)
                for n in range(2):
                    for a, b, s in ((0, P, QSCALE), (P, 2 * P, 1.0), (2 * P, 2 * P + CB, QSCALE),
                                    (2 * P + CB, 3 * C, 1.0)):
                        dve.tensor_scalar(qkv_hi[:, n, a:b], raw_qkv[:, n, a:b], lncol[:, n:n + 1], s,
                                          ALU.mult, ALU.mult)
                    dve.tensor_scalar(w1_hi[:, n, :], raw_w1[:, n, :], lncol[:, 4 + n:5 + n], None, ALU.mult)
                dve.wait_ge(prep_mm, 1)
                for n in range(2):
                    for a, b, s in ((0, P, QSCALE), (P, 2 * P, 1.0), (2 * P, 2 * P + CB, QSCALE),
                                    (2 * P + CB, 3 * C, 1.0)):
                        dve.tensor_scalar(raw_qkv[:, n, a:b], raw_qkv[:, n, a:b], lncol[:, n:n + 1], s,
                                          ALU.mult, ALU.mult)
                    last = dve.tensor_scalar(raw_w1[:, n, :], raw_w1[:, n, :], lncol[:, 4 + n:5 + n], None,
                                             ALU.mult)
                last.then_inc(prep_w, 1)
                dve.wait_ge(prep_w, 1)
                dve.tensor_tensor(qkv_lo[:], raw_qkv[:], qkv_hi[:], ALU.subtract)
                dve.tensor_tensor(w1_lo[:], raw_w1[:], w1_hi[:], ALU.subtract)
                dve.tensor_tensor(bias_qkv[:, 0:4], PT0[:, 0:4], bqkv_col[:, 0:4], ALU.add)
                dve.tensor_tensor(bias_qkv[0:CB, 4:5], PT0[0:CB, 4:5], bqkv_col[0:CB, 4:5], ALU.add)
                dve.tensor_tensor(bias_hid[:], PT1[:, 0:NH1], b1_col[:], ALU.add).then_inc(prep_w, 1)
                dve.wait_ge(prep_w, 2)
                dve.tensor_scalar(bias_qkv[:, 0:1], bias_qkv[:, 0:1], QSCALE, None, ALU.mult)
                dve.tensor_scalar(bias_qkv[0:CB, 2:3], bias_qkv[0:CB, 2:3], QSCALE, None,
                                  ALU.mult).then_inc(prep_bias, 1)
                for kind in range(2):
                    for h in range(HEADS):
                        last = dve.tensor_tensor(bias_att[:, kind, h, :], rel_sb[:, h, :],
                                                 mask_sb[:, kind, :], ALU.add)
                last.then_inc(prep_att, 1)

            def moments(g, n, src):
                for t in range(NT):
                    last = dve.bn_stats(stats[:, n, t, :], src[:, t, :])
                last.then_inc(ln_stats[n], 1)
                wait_alone(dve, ln_stats[n], g + 1)
                for t in range(NT):
                    last = dve.bn_aggr(mv[:, n, t, :], stats[:, n, t, :])
                last.then_inc(ln_mv[n], 1)

            def normalise(g, n, src):
                after(dve, turned[n], 2 * g)
                dve.wait_ge(ln_rstd[n], g + 1)
                for t in range(NT):
                    last = dve.tensor_scalar(xn[:, n, t, 0:C], src[:, t, :], mv[:, n, t, 0:1],
                                             rstd[:, n, t:t + 1], ALU.subtract, ALU.mult)
                last.then_inc(ln_norm[n], 1)
                dve.wait_ge(ln_norm[n], g + 1)
                dve.tensor_copy(xn[:, n, :, C:2 * P], xn[:, n, :, P:C]).then_inc(ln_dup[n], 1)

            def moments1(g):
                dve.wait_ge(x_in, 32 * g + 32)
                moments(g, 0, xin)

            def copy_probs(g, n):
                u = (2, 0, 1)[n]
                dve.wait_ge(pt_mm, 3 * g + 1 + n)
                dve.tensor_copy(pT[WT:P, 2 * u:2 * u + 2, :, WT:P].rearrange("p h t q -> p (h t) q"),
                                pt_bank[n][WT:P, :].rearrange("p (x q) -> p x q", q=WT)).then_inc(pt_set[1], 1)

            def back(g):
                dve.wait_ge(pv_mm, g + 1)
                for dst, src in zip(ww_cols(attT[:, 0, :]), win_cols(PV0)):
                    last = dve.tensor_scalar(dst, src, bias_qkv[:, 3:4], None, ALU.add)
                last.then_inc(att_set[0], 1)

            def residual(g):
                after(dve, x2b_set, g)
                dve.wait_ge(xres_set, g + 1)
                for n in range(2):
                    dve.wait_ge(proj_mm, 2 * g + 1 + n)
                    dve.tensor_tensor(x2[:, 2 * n:2 * n + 2, :], xres[:, 2 * n:2 * n + 2, :],
                                      pj_bank[n][:, 0:2 * C].rearrange("p (t c) -> p t c", c=C),
                                      ALU.add).then_inc(x2_set, 1)
                dve.wait_ge(x2_set, 2 * g + 2)
                moments(g, 1, x2)
                normalise(g, 1, x2)

            def low1(g):
                dve.wait_ge(hi_set[0], 2 * g + 1)
                for (d, s, h) in zip(win_cols(hA_lo[:]), ww_cols(TA1), win_cols(hA_hi[:])):
                    last = dve.tensor_tensor(d, s, h, ALU.subtract)
                last.then_inc(lo_set[0], 1)
                dve.wait_ge(hi_set[0], 2 * g + 2)
                for (d, s, h) in zip(win_cols(hB[CB:P, :]), ww_cols(TB1[CB:P, :]), win_cols(hB[CB:P, :])):
                    last = dve.tensor_tensor(d, s, h, ALU.subtract)
                last.then_inc(lo_set[0], 1)

            def values(g):
                for n in range(2):
                    dve.wait_ge(v_mm, 2 * g + 1 + n)
                    dve.tensor_copy(vt[:, 2 * n:2 * n + 2, :].rearrange("p t c -> p (t c)"),
                                    v_bank[n][:, 0:2 * C]).then_inc(v_set, 1)

            def softmax(g):
                last_row = ((g & 7) + 1) >> 3
                for n, (src, hs) in enumerate((
                    (scores[:, 2:4, 0:4 * WT], slice(4, 6)),
                    (scores[:, 0:2, :].rearrange("p b (s k) -> p (b s) k", s=2), slice(0, 4)),
                )):
                    dve.wait_ge(s_mm, 2 * g + 1 + n)
                    dve.tensor_tensor(prob[:, hs, :], src, bias_att[:, last_row, hs, :],
                                      ALU.add).then_inc(s_biased, 1)
                    rows = slice(hs.start * 4, hs.stop * 4)
                    p3 = prob[:, hs, :].rearrange("p h (w k) -> p (h w) k", k=WT)
                    dve.wait_ge(s_biased, 2 * g + 1 + n)
                    dve.tensor_reduce(pmax[:, rows], p3, AX_X, ALU.max).then_inc(s_max, 1)
                    dve.wait_ge(s_max, 2 * g + 1 + n)
                    dve.tensor_tensor(p3, p3, pmax[:, rows].unsqueeze(2).broadcast_to([P, rows.stop - rows.start, WT]),
                                      ALU.subtract).then_inc(s_less, 1)

            def sums(g):
                for n, hs in enumerate((slice(4, 6), slice(0, 4))):
                    rows = slice(hs.start * 4, hs.stop * 4)
                    p3 = prob[:, hs, :].rearrange("p h (w k) -> p (h w) k", k=WT)
                    dve.wait_ge(p_exp, 2 * g + 1 + n)
                    dve.tensor_reduce(psum_[:, rows], p3, AX_X, ALU.add).then_inc(p_sum, 1)
                    dve.wait_ge(p_sum, 2 * g + 1 + n)
                    dve.reciprocal(prec[:, rows], psum_[:, rows]).then_inc(p_rec, 1)

            def mlp_lo(g):
                dve.wait_ge(hi_set[1], 2 * g + 1)
                dve.tensor_tensor(mA_lo[:], TA2, mA_hi[:], ALU.subtract).then_inc(lo_set[1], 1)
                dve.wait_ge(hi_set[1], 2 * g + 2)
                dve.tensor_tensor(mB[CB:P, :], TB2[CB:P, :], mB[CB:P, :], ALU.subtract).then_inc(lo_set[1], 1)

            def result(g, n):
                if n == 0:
                    dve.wait_ge(x2b_set, g + 1)
                    after(dve, y_out, 32 * g)
                dve.wait_ge(y_mm, 2 * g + 1 + n)
                dve.tensor_tensor(yt[:, 2 * n:2 * n + 2, :], x2b[:, 2 * n:2 * n + 2, :],
                                  y_bank[n][:, 0:2 * C].rearrange("p (t c) -> p t c", c=C),
                                  ALU.add).then_inc(y_set, 1)

            prep()
            moments1(0)
            normalise(0, 0, xin)
            low1(0)
            values(0)
            dve.wait_ge(prep_att, 1)
            softmax(0)
            moments1(1)
            sums(0)
            normalise(1, 0, xin)
            for n in range(3):
                copy_probs(0, n)
            back(0)
            low1(1)
            residual(0)
            values(1)
            mlp_lo(0)
            softmax(1)
            moments1(2)
            sums(1)
            normalise(2, 0, xin)
            result(0, 0)
            copy_probs(1, 0)
            result(0, 1)
            copy_probs(1, 1)
            copy_probs(1, 2)
            with dve.Fori(1, G - 2) as g:
                back(g)
                low1(g + 1)
                residual(g)
                values(g + 1)
                mlp_lo(g)
                softmax(g + 1)
                moments1(g + 2)
                sums(g + 1)
                normalise(g + 2, 0, xin)
                result(g, 0)
                copy_probs(g + 1, 0)
                result(g, 1)
                copy_probs(g + 1, 1)
                copy_probs(g + 1, 2)
            back(G - 2)
            low1(G - 1)
            residual(G - 2)
            values(G - 1)
            mlp_lo(G - 2)
            softmax(G - 1)
            sums(G - 1)
            result(G - 2, 0)
            copy_probs(G - 1, 0)
            result(G - 2, 1)
            copy_probs(G - 1, 1)
            copy_probs(G - 1, 2)
            back(G - 1)
            residual(G - 1)
            mlp_lo(G - 1)
            result(G - 1, 0)
            result(G - 1, 1)

        @block.gpsimd
        def _(pool):
            def scale(g, n):
                wait_alone(pool, ln_mv[n], g + 1)
                pool.tensor_scalar(veps[:, n, :], mv[:, n, :, 1], EPS, None, ALU.add).then_inc(ln_eps[n], 1)
                pool.wait_ge(ln_eps[n], g + 1)
                pool.tensor_tensor(rstd[:, n, :], veps[:, n, :], mhalf[:], ALU.pow).then_inc(ln_rstd[n], 1)

            def keep_x(g):
                pool.wait_ge(x_in, 32 * g + 32)
                after(pool, x2_set, 2 * g)
                pool.tensor_tensor(xres[:], xin[:], bproj_all[:].unsqueeze(1).broadcast_to([P, NT, C]),
                                   ALU.add).then_inc(xres_set, 1)

            def keep_x2(g):
                after(pool, y_set, 2 * g)
                pool.tensor_tensor(x2b[:], x2[:], b2_all[:].unsqueeze(1).broadcast_to([P, NT, C]),
                                   ALU.add).then_inc(x2b_set, 1)

            def probs(g):
                for n, hs in enumerate((slice(4, 6), slice(0, 4))):
                    rows = slice(hs.start * 4, hs.stop * 4)
                    p3 = prob[:, hs, :].rearrange("p h (w k) -> p (h w) k", k=WT)
                    pool.wait_ge(p_rec, 2 * g + 1 + n)
                    pool.tensor_tensor(p3, p3, prec[:, rows].unsqueeze(2).broadcast_to([P, rows.stop - rows.start, WT]),
                                       ALU.mult).then_inc(p_norm, 1)

            pool.wait_ge(prep_half, 1)
            scale(0, 0)
            pool.wait_ge(consts_in, 12 * 16)
            keep_x(0)
            scale(1, 0)
            probs(0)
            scale(0, 1)
            keep_x2(0)
            keep_x(1)
            scale(2, 0)
            probs(1)
            with pool.Fori(1, G - 2) as g:
                scale(g, 1)
                keep_x2(g)
                keep_x(g + 1)
                scale(g + 2, 0)
                probs(g + 1)
            scale(G - 2, 1)
            keep_x2(G - 2)
            keep_x(G - 1)
            probs(G - 1)
            scale(G - 1, 1)
            keep_x2(G - 1)


def _token(win_kind):
    i, j = np.meshgrid(np.arange(WIN), np.arange(WIN), indexing="ij")
    if win_kind == "wrapped":
        j = (j + SHIFT) % WIN
    return i.ravel(), j.ravel()


def _places():
    iq = np.zeros((P, 4 * WT), np.int64)
    jq, ik, jk, wrap = iq.copy(), iq.copy(), iq.copy(), np.zeros((P, 4 * WT), bool)
    for tp in range(2):
        for tt in range(2):
            for w in range(2):
                last = 4 * tt + 2 * tp + w == NWIN - 1
                i, j = _token("wrapped" if last else "regular")
                rows, cols = slice(WT * tp, WT * (tp + 1)), slice((2 * tt + w) * WT, (2 * tt + w + 1) * WT)
                iq[rows, cols], jq[rows, cols] = i[:, None], j[:, None]
                ik[rows, cols], jk[rows, cols] = i[None, :], j[None, :]
                wrap[rows, cols] = last
    return iq, jq, ik, jk, wrap


def _lay_out(inputs):
    a = {k: np.asarray(v) for k, v in inputs.items()}
    f = np.float32
    p = "L0_conv_"

    def two_parts(w):
        return np.ascontiguousarray(np.stack([w[:P], np.concatenate([w[P:], w[P:]])], 1))

    def two_cols(v):
        return np.stack([v[:P], np.concatenate([v[P:], v[P:]])], 1)

    order = np.concatenate([np.arange(0, P), np.arange(C, C + P), np.arange(P, C), np.arange(C + P, 2 * C),
                            np.arange(2 * C, 3 * C)])
    bq = a[p + "b_qkv"][order]
    zeros = np.zeros(CB, f)
    bqkv = np.stack([bq[0:P], bq[P:2 * P], bq[2 * P:3 * P], bq[2 * C:2 * C + P],
                     np.concatenate([bq[2 * C + P:], zeros])], 1)
    ln = np.concatenate([two_cols(a[p + n]) for n in ("g1", "b1", "g2", "b2")], 1)
    iq, jq, ik, jk, wrap = _places()
    rel = a[p + "rel_pos"][HEAD_AT][:, iq - ik + WIN - 1, jq - jk + WIN - 1].transpose(1, 0, 2)
    across_cols = wrap & ((jq < SHIFT) != (jk < SHIFT))
    across_rows = (iq < SHIFT) != (ik < SHIFT)
    mask = np.stack([across_cols, across_cols | across_rows], 1).astype(f) * f(MASKED)
    c = np.ascontiguousarray
    return {
        "x": c(a["x"]), "wqkv": two_parts(a[p + "w_qkv"][:, order]), "bqkv": c(bqkv), "ln": c(ln),
        "rel": c(rel), "mask": c(mask), "wproj": two_parts(a[p + "w_proj"]), "bproj": c(a[p + "b_proj"]),
        "w1": two_parts(a[p + "w_mlp1"]), "b1": c(a[p + "b_mlp1"].reshape(NH1, P).T),
        "w2": c(a[p + "w_mlp2"].reshape(NH1, P, C).transpose(1, 0, 2)), "b2": c(a[p + "b_mlp2"]),
        "ident": np.eye(P, dtype=f),
    }


def kernel(**inputs):
    import concourse.bacc as bacc
    from concourse.bass_utils import run_bass_kernel_spmd

    arrays = _lay_out(inputs)
    nc = bacc.Bacc("TRN2", target_bir_lowering=False, num_devices=1)
    args = {k: nc.dram_tensor(f"in_{k}", v.shape, F32, kind="ExternalInput").ap() for k, v in arrays.items()}
    out = nc.dram_tensor("out", (B, H, W, C), F32, kind="ExternalOutput").ap()
    swin_block(nc, out=out, **args)
    r = run_bass_kernel_spmd(nc, [{f"in_{k}": v for k, v in arrays.items()}], core_ids=[0])
    return r.results[0]["out"]
```

```python
from contextlib import ExitStack

import numpy as np

import concourse.bass as bass
from concourse import mybir

F32 = mybir.dt.float32
F32R = mybir.dt.float32r
ALU = mybir.AluOpType
ACT = mybir.ActivationFunctionType
AX_X = mybir.AxisListType.X

P = 128
B, H, W, C = 16, 64, 64, 192
HEADS, HD, WIN = 6, 32, 8
SHIFT = WIN // 2
WT = WIN * WIN
NWIN = W // WIN
T = WIN * W
NT = T // P
PLACE = [t % 2 * (NT // 2) + t // 2 for t in range(NT)]
ROWS = [2 * t + r for t in (0, 2, 1, 3) for r in range(2)]
G = B * H // WIN
GPI = H // WIN
CB = C - P
HID = 4 * C
NH1 = HID // P
EPS = 1e-5
QSCALE = HD ** -0.5
MASKED = -1e30
HEAD_SETS = (slice(0, 4), slice(4, 6))


def swin_block(nc, x, wqkv, bqkv, ln, rel, mask, wproj, bproj, w1, b1, w2, b2, ident, out):
    with ExitStack() as ctx:
        def sb(name, shape, dt=F32):
            return ctx.enter_context(nc.sbuf_tensor(name, shape, dt))

        def sem(name):
            return ctx.enter_context(nc.semaphore(name))

        scores = ctx.enter_context(nc.psum_tensor("scores", [P, 4, 512], F32))
        ring = ctx.enter_context(nc.psum_tensor("ring", [P, 4, 512], F32))
        TA2, TB2 = scores[:, 2, :], scores[:, 3, :]
        proj_bank = scores
        (PV0, PV1, TA1, TB1, QK0, QK1, QK2, V0, V1, V2, V3, Y0, Y1, Y2, Y3,
         H0, H1, H2, H3, PT0, PT1, PT2, H4, H5) = [ring[:, i % 4, :] for i in range(24)]
        qk_bank, v_bank, y_bank = (QK0, QK1, QK2), (V0, V1, V2, V3), (Y0, Y1, Y2, Y3)
        hid_bank, pt_bank = (H0, H1, H2, H3, H4, H5), (PT0, PT1, PT2)

        eye = sb("eye", [P, P])
        raw_qkv = sb("raw_qkv", [P, 2, 3 * C])
        raw_w1 = sb("raw_w1", [P, 2, HID])
        lncol = sb("lncol", [P, 8])
        qkv_w = sb("qkv_w", [P, 2, 2, 3 * C], F32R)
        qkv_hi, qkv_lo = qkv_w[:, :, 0, :], qkv_w[:, :, 1, :]
        w1_hi = sb("w1_hi", [P, 2, HID], F32R)
        w1_lo = sb("w1_lo", [P, 2, HID], F32R)
        raw_w2 = sb("raw_w2", [P, NH1, C])
        w2_w = sb("w2_w", [P, NH1, 2, C], F32R)
        raw_wp = sb("raw_wp", [P, 2, C])
        wp_w = sb("wp_w", [P, 2, 2, C], F32R)
        bqkv_col = sb("bqkv_col", [P, 5])
        bias_qkv = sb("bias_qkv", [P, 5])
        b1_col = sb("b1_col", [P, NH1])
        bias_hid = sb("bias_hid", [P, NH1])
        bproj_all = sb("bproj_all", [P, C])
        b2_all = sb("b2_all", [P, C])
        rel_sb = sb("rel_sb", [P, HEADS, 4 * WT])
        mask_sb = sb("mask_sb", [P, 2, 4 * WT])
        bias_att = sb("bias_att", [P, 2, HEADS, 4 * WT])
        bv_cols = sb("bv_cols", [P, 2, P])
        mhalf = sb("mhalf", [P, NT])

        xin = sb("xin", [P, NT, C])
        xres = sb("xres", [P, NT, C])
        stats = sb("stats", [P, 2, NT, 6])
        mv = sb("mv", [P, 2, NT, 2])
        veps = sb("veps", [P, 2, NT])
        rstd = sb("rstd", [P, 2, NT])
        xn = sb("xn", [P, 2, NT, C])
        xnB = sb("xnB", [P, 2, NT, CB])
        hA_hi = sb("hA_hi", [P, T], F32R)
        hA_lo = sb("hA_lo", [P, T], F32R)
        hB = sb("hB", [P, T], F32R)
        mA_hi = sb("mA_hi", [P, T], F32R)
        mA_lo = sb("mA_lo", [P, T], F32R)
        mB = sb("mB", [P, T], F32R)
        qT = sb("qT", [P, 2, T])
        kT = sb("kT", [P, 2, T])
        vt = sb("vt", [P, NT, C])
        prob = sb("prob", [P, HEADS, 4 * WT])
        pmax = sb("pmax", [P, HEADS * 4])
        psum_ = sb("psum_", [P, HEADS * 4])
        prec = sb("prec", [P, HEADS * 4])
        pT = sb("pT", [P, HEADS, NT, P])
        attA_hi = sb("attA_hi", [P, T], F32R)
        attA_lo = sb("attA_lo", [P, T], F32R)
        attB = sb("attB", [P, T], F32R)
        x2 = sb("x2", [P, NT, C])
        x2b = sb("x2b", [P, NT, C])
        hid = sb("hid", [P, NH1, T])
        hid_hi = sb("hid_hi", [P, NH1, T], F32R)
        hid_lo = sb("hid_lo", [P, NH1, T], F32R)
        yh = sb("yh", [P, NT, C])
        yt = sb("yt", [P, NT, C])

        consts_in = [sem("consts_in"), sem("consts_in_later")]
        prep_half = sem("prep_half")
        prep_qkv_mm = sem("prep_qkv_mm")
        prep_proj_mm = sem("prep_proj_mm")
        prep_hid_mm = sem("prep_hid_mm")
        prep_gained = sem("prep_gained")
        prep_qkv = sem("prep_qkv")
        prep_bias = sem("prep_bias")
        prep_proj = sem("prep_proj")
        prep_rest = sem("prep_rest")
        prep_hid = sem("prep_hid")
        prep_att = sem("prep_att")
        passed = sem("passed")
        x_in = sem("x_in")
        ln_stats = [sem("ln1_stats"), sem("ln2_stats")]
        ln_mv = [sem("ln1_mv"), sem("ln2_mv")]
        ln_eps = [sem("ln1_eps"), sem("ln2_eps")]
        ln_rstd = [sem("ln1_rstd"), sem("ln2_rstd")]
        ln_norm = [sem("ln1_norm"), sem("ln2_norm")]
        xres_set = sem("xres_set")
        x2b_set = sem("x2b_set")
        turned = [sem("turned1"), sem("turned2")]
        hi_set = [sem("hi1_set"), sem("hi2_set")]
        lo_set = [sem("lo1_set"), sem("lo2_set")]
        qk_mm = sem("qk_mm")
        qk_set = sem("qk_set")
        v_mm = sem("v_mm")
        v_part = sem("v_part")
        v_set = sem("v_set")
        s_mm = sem("s_mm")
        s_biased = sem("s_biased")
        s_max = sem("s_max")
        s_less = sem("s_less")
        p_exp = sem("p_exp")
        p_sum = sem("p_sum")
        p_rec = sem("p_rec")
        p_norm = sem("p_norm")
        pt_mm = sem("pt_mm")
        pt_set = [sem("pt_set0"), sem("pt_set1")]
        pt_zero = sem("pt_zero")
        pv_mm = sem("pv_mm")
        att_split = [sem("att_hi_set"), sem("att_lo_set")]
        proj_mm = sem("proj_mm")
        x2_part = sem("x2_part")
        x2_set = sem("x2_set")
        hid_mm = sem("hid_mm")
        hid_set = sem("hid_set")
        hid_split = [sem("hid_hi_set"), sem("hid_lo_set")]
        y_mm = sem("y_mm")
        y_half = [sem("y_half0_read"), sem("y_half1_read")]
        y_set = sem("y_set")
        y_out = sem("y_out")

        x_halves = x.rearrange("b (r i) w c -> (b r) (i w) c", i=SHIFT)
        out_halves = out.rearrange("b (r i) w c -> (b r) (i w) c", i=SHIFT)
        tiles_of_half = SHIFT * W // P

        def half_at(g, half):
            at = (g >> 3) * (2 * GPI) + ((2 * (g & 7) + 1 + half) & (2 * GPI - 1))
            return at if isinstance(g, int) else nc.s_assert_within(at, 0, 2 * GPI * B - 1)

        def after(eng, s, value):
            if isinstance(value, int) and value <= 0:
                return
            eng.wait_ge(s, value)

        def wait_alone(eng, s, value):
            eng.wait_ge(s, value)
            if not isinstance(value, int):
                eng.sem_inc(passed, 1)

        def at_place(t):
            return slice(PLACE[t] * P, (PLACE[t] + 1) * P)

        def ww_cols(ap):
            rows = ap.rearrange("p (i c) -> p i c", c=W)
            regular = rows[:, :, SHIFT:W - SHIFT].rearrange("p i (w j) -> p w i j", j=WIN)
            ends = rows.rearrange("p i (h j) -> p i h j", j=SHIFT)
            wrapped = ends[:, :, 0:2 * NWIN:2 * NWIN - 1, :]
            return regular, wrapped

        def win_cols(ap, rows=slice(0, WIN)):
            wins = ap.rearrange("p (w i j) -> p w i j", w=NWIN, j=WIN)
            regular = wins[:, 0:NWIN - 1, rows]
            wrapped = wins[:, NWIN - 1, rows].rearrange("p i (h j) -> p i h j", j=SHIFT)
            return regular, wrapped

        halves = (slice(0, CB), slice(CB, P))
        b_parts = tuple((halves[u], halves[1 - u], slice(u * T // 2, (u + 1) * T // 2),
                         slice(u * WIN // 2, (u + 1) * WIN // 2)) for u in range(2))

        block = ctx.enter_context(nc.Block())

        @block.sync
        def _(sp):
            def load(g):
                after(sp, ln_norm[0], 2 * g)
                after(sp, xres_set, g)
                for half in range(2):
                    sp.dma_start(
                        xin[:, half * tiles_of_half:(half + 1) * tiles_of_half, :],
                        x_halves[half_at(g, half)].rearrange("(t p) c -> p t c", p=P),
                    ).then_inc(x_in, 16)

            def store(g):
                for half in range(2):
                    at = half_at(g, half)
                    wait_alone(sp, y_set, NT * g + 2 * (half + 1))
                    sp.dma_start(
                        out_halves[at].rearrange("(t p) c -> p t c", p=P),
                        yt[:, half * tiles_of_half:(half + 1) * tiles_of_half, :],
                    ).then_inc(y_out, 16)

            load(0)
            for n, arrays in enumerate((
                ((lncol[:], ln), (raw_qkv[:], wqkv), (bqkv_col[:], bqkv), (eye[:], ident),
                 (raw_wp[:], wproj), (bproj_all[:], bproj.partition_broadcast(P))),
                ((rel_sb[:], rel), (mask_sb[:], mask), (raw_w1[:], w1), (b1_col[:], b1),
                 (raw_w2[:], w2), (b2_all[:], b2.partition_broadcast(P))),
            )):
                for dst, src in arrays:
                    sp.dma_start(dst, src).then_inc(consts_in[n], 16)
            load(1)
            load(2)
            with sp.Fori(1, G - 2) as g:
                load(g + 2)
                store(g - 1)
            store(G - 3)
            store(G - 2)
            store(G - 1)
            sp.wait_ge(y_out, 32 * G)

        @block.tensor
        def _(pe):
            def mm(dst, lhs, rhs, first=True, last=True):
                return pe.matmul(dst, lhs, rhs, start=first, stop=last)

            def prep_qkv_bias():
                pe.wait_ge(consts_in[0], 6 * 16)
                for col, a, n, at in ((0, 0, P, 0), (1, P, P, 0), (2, 2 * P, CB, 0), (2, 2 * P + CB, CB, CB),
                                      (3, 2 * C, P, 0), (4, 2 * C + P, CB, 0)):
                    dst = scores[at:at + n, 0, col:col + 1]
                    mm(dst, raw_qkv[:, 0, a:a + n], lncol[:, 2:3], True, False)
                    last = mm(dst, raw_qkv[0:CB, 1, a:a + n], lncol[0:CB, 3:4], False, True)
                last.then_inc(prep_qkv_mm, 1)

            def prep_proj_bias():
                pe.wait_ge(prep_bias, 2)
                dst = scores[:, 1, 0:C]
                mm(dst, bv_cols[:, 0, :], raw_wp[:, 0, :], True, False)
                mm(dst, bv_cols[0:CB, 1, :], raw_wp[0:CB, 1, :], False, True).then_inc(prep_proj_mm, 1)

            def prep_hid_bias():
                pe.wait_ge(consts_in[1], 6 * 16)
                for m in range(NH1):
                    dst = scores[:, 2, m:m + 1]
                    mm(dst, raw_w1[:, 0, m * P:(m + 1) * P], lncol[:, 6:7], True, False)
                    last = mm(dst, raw_w1[0:CB, 1, m * P:(m + 1) * P], lncol[0:CB, 7:8], False, True)
                last.then_inc(prep_hid_mm, 1)

            def turn(g, n, bank_a, bank_b):
                pe.wait_ge(ln_norm[n], 2 * g + 1)
                for t in range(NT):
                    last = pe.transpose(bank_a[:, at_place(t)], xn[:, n, t, 0:P], eye[:])
                last.then_inc(turned[n], 1)
                pe.wait_ge(ln_norm[n], 2 * g + 2)
                for u in range(NT // 2):
                    last = pe.transpose(bank_b[:, u * P:(u + 1) * P],
                                        xnB[:, n, 2 * u:2 * u + 2, :].rearrange("p t c -> p (t c)"), eye[:])
                last.then_inc(turned[n], 1)

            def products(banks, ms, w_hi, w_lo, a_hi, a_lo, b, n, g):
                for m in ms:
                    cols = slice(m * P, (m + 1) * P)
                    if m == 0:
                        pe.wait_ge(hi_set[n], 2 * g + 1)
                    if n == 1 and m < NT:
                        after(pe, y_half[0], NT * (g - 1) + m + 1)
                        after(pe, y_half[1], NT * (g - 1) + m + 1)
                    mm(banks[m], w_hi[:, 0, cols], a_hi, True, False)
                    mm(banks[m], w_lo[:, 0, cols], a_hi, False, False)
                    if m == 0:
                        pe.wait_ge(lo_set[n], 2 * g + 1)
                    mm(banks[m], w_hi[:, 0, cols], a_lo, False, False)
                for m in ms:
                    cols = slice(m * P, (m + 1) * P)
                    if m == 0:
                        pe.wait_ge(hi_set[n], 2 * g + 2)
                        pe.wait_ge(lo_set[n], 2 * g + 2)
                    mm(banks[m], w_hi[:, 1, cols], b, False, False)
                    mm(banks[m], w_lo[:, 1, cols], b, False, True).then_inc((qk_mm, hid_mm)[n], 1)

            def turn1(g):
                after(pe, hid_set, NH1 * (g - 1))
                turn(g, 0, TA1, TB1)

            def v_tile(t):
                cols, at = slice(2 * C, 3 * C), slice(t * P, (t + 1) * P)
                both = v_bank[t][:, 0:2 * C]
                mm(both, hA_hi[:, at], qkv_w[:, 0, :, cols], True, False)
                mm(both, hB[:, at], qkv_w[:, 1, :, cols], False, False)
                return mm(both[:, 0:C], hA_lo[:, at], qkv_hi[:, 0, cols], False, True)

            def score_part(heads, tt, w):
                for tp in range(2):
                    for h in heads:
                        ww = 4 * tt + 2 * tp + w
                        r = h % 4
                        rows = slice(HD * r, HD * (r + 1))
                        at = (h // 4) * 4 * WT + (2 * tt + w) * WT
                        last = mm(scores[WT * tp:WT * (tp + 1), r, at:at + WT],
                                  qT[rows, h // 4, ww * WT:(ww + 1) * WT],
                                  kT[rows, h // 4, ww * WT:(ww + 1) * WT])
                return last

            def front(g):
                for ms in ((0, 1), (2,)):
                    products(qk_bank, ms, qkv_hi, qkv_lo, hA_hi[:], hA_lo[:], hB[:], 0, g)
                pe.wait_ge(qk_set, 3 * g + 2)
                after(pe, x2_set, 2 * g)
                score_part((0, 1, 2, 3), 0, 0)
                score_part((0, 1, 2, 3), 0, 1)
                for t in range(3):
                    v_tile(t).then_inc(v_mm, 1)
                score_part((0, 1, 2, 3), 1, 0)
                score_part((0, 1, 2, 3), 1, 1).then_inc(s_mm, 1)
                pe.wait_ge(qk_set, 3 * g + 3)
                v_tile(3).then_inc(v_mm, 1)

            def front_end(g):
                pe.wait_ge(s_biased, 2 * g + 1)
                for t in range(NT):
                    last = score_part((4, 5), t // 2, t % 2)
                last.then_inc(s_mm, 1)

            def turn_probs(g):
                for n in range(3):
                    pe.wait_ge(p_norm, 2 * g + 1 + n // 2)
                    after(pe, hid_set, NH1 * (g - 1) + 1 + n)
                    for v in range(2):
                        for tt in range(2):
                            last = pe.transpose(
                                pt_bank[n][:, (2 * v + tt) * P:(2 * v + tt + 1) * P],
                                prob[:, 2 * n + v, tt * 2 * WT:(tt + 1) * 2 * WT], eye[:])
                    last.then_inc(pt_mm, 1)

            def back(g):
                for heads, n in ((range(4), 2), (range(4, HEADS), 3)):
                    pe.wait_ge(pt_set[0], 3 * g + n)
                    wait_alone(pe, pt_set[1], 3 * g + n)
                    if n == 2:
                        pe.wait_ge(v_set, NT * g + NT)
                    for t in range(NT):
                        for h in heads:
                            last = mm((PV0, PV1)[h // 4][HD * (h % 4):HD * (h % 4 + 1), t * P:(t + 1) * P],
                                      vt[:, t, h * HD:(h + 1) * HD], pT[:, h, t, :])
                    last.then_inc(pv_mm, 1)

            def project(g):
                at = [at_place(t) for t in range(NT)]
                pe.wait_ge(att_split[0], 2 * g + 1)
                for t in range(NT):
                    mm(proj_bank[:, t, 0:2 * C], attA_hi[:, at[t]], wp_w[:, 0, :, :], True, False)
                pe.wait_ge(att_split[1], 2 * g + 1)
                for t in range(NT):
                    mm(proj_bank[:, t, 0:C], attA_lo[:, at[t]], wp_w[:, 0, 0, :], False, False)
                pe.wait_ge(att_split[0], 2 * g + 2)
                pe.wait_ge(att_split[1], 2 * g + 2)
                for t in range(NT):
                    last = mm(proj_bank[:, t, 0:2 * C], attB[:, at[t]], wp_w[:, 1, :, :], False, True)
                    if t % 2:
                        last.then_inc(proj_mm, 1)

            def y_tile(g, t):
                at = at_place(t)
                both = y_bank[t][:, 0:2 * C]
                pe.wait_ge(hid_split[0], NH1 * g + NH1)
                for m in range(NH1):
                    mm(both, hid_hi[:, m, at], w2_w[:, m, :, :], m == 0, False)
                pe.wait_ge(hid_split[1], NH1 * g + NH1)
                for m in range(NH1):
                    last = mm(both[:, 0:C], hid_lo[:, m, at], w2_w[:, m, 0, :], False, m == NH1 - 1)
                last.then_inc(y_mm, 1)

            def mlp2(g, front_ran):
                for t in range(NT):
                    if t == NT - 1:
                        turn(g + 1, 1, TA2, TB2)
                    if front_ran:
                        pe.wait_ge(v_set, NT * g + 2 * NT + t + 1)
                    y_tile(g, t)
                    if front_ran and t == 0:
                        front_end(g + 2)

            def mlp1(g, woven):
                for ms in ((0, 1), (2,), (3,), (4,), (5,)):
                    if 4 in ms:
                        if woven:
                            turn_probs(g + 1)
                        pe.wait_ge(hid_set, NH1 * g + 4)
                    if 5 in ms and woven:
                        pe.wait_ge(pt_set[0], 3 * g + 4)
                        wait_alone(pe, pt_set[1], 3 * g + 4)
                    products(hid_bank, ms, w1_hi, w1_lo, mA_hi[:], mA_lo[:], mB[:], 1, g)

            prep_qkv_bias()
            turn1(0)
            prep_proj_bias()
            pe.wait_ge(prep_qkv, 1)
            pe.wait_ge(prep_proj, 1)
            front(0)
            front_end(0)
            prep_hid_bias()
            turn_probs(0)
            pe.wait_ge(prep_rest, 1)
            pe.wait_ge(prep_hid, 1)
            back(0)
            turn1(1)
            project(0)
            front(1)
            front_end(1)
            pe.wait_ge(v_set, 2 * NT)
            turn(0, 1, TA2, TB2)
            mlp1(0, True)
            with pe.Fori(1, G - 1) as g:
                back(g)
                turn1(g + 1)
                project(g)
                front(g + 1)
                mlp2(g - 1, True)
                mlp1(g, True)
            back(G - 1)
            project(G - 1)
            mlp2(G - 2, False)
            mlp1(G - 1, False)
            for t in range(NT):
                y_tile(G - 1, t)

        @block.scalar
        def _(act):
            def copy_probs(g):
                for n in range(3):
                    act.wait_ge(pt_mm, 3 * g + 1 + n)
                    act.copy(pT[0:WT, 2 * n:2 * n + 2, :, 0:WT].rearrange("p h t q -> p (h t) q"),
                             pt_bank[n][0:WT, :].rearrange("p (x q) -> p x q", q=WT)).then_inc(pt_set[0], 1)

            def back(g):
                for n, (bank, d) in enumerate(((PV0, attA_hi[:]), (PV1[0:CB, :], attB[0:CB, :]))):
                    act.wait_ge(pv_mm, 2 * g + 1 + n)
                    for dst, src in zip(ww_cols(d), win_cols(bank)):
                        last = act.copy(dst, src)
                    last.then_inc(att_split[0], 1)

            def high(g, m):
                act.wait_ge(hid_set, NH1 * g + m + 1)
                act.copy(hid_hi[:, m, :], hid[:, m, :]).then_inc(hid_split[0], 1)

            def front(g):
                act.wait_ge(turned[0], 2 * g + 1)
                for dst, src in zip(win_cols(hA_hi[:]), ww_cols(TA1)):
                    last = act.copy(dst, src)
                last.then_inc(hi_set[0], 1)
                act.wait_ge(turned[0], 2 * g + 2)
                for high_at, _, _, rows in b_parts:
                    for dst, src in zip(win_cols(hB[high_at, :], rows), ww_cols(TB1[high_at, 0:T // 2])):
                        last = act.copy(dst, src)
                last.then_inc(hi_set[0], 1)
                if not isinstance(g, int) or g > 1:
                    high(g - 2, NH1 - 2)
                    high(g - 2, NH1 - 1)
                for m in range(3):
                    act.wait_ge(qk_mm, 3 * g + 1 + m)
                    if m < 2:
                        act.activation((qT, kT)[m][:, 0, :], qk_bank[m], ACT.Identity,
                                       bias=bias_qkv[:, m:m + 1]).then_inc(qk_set, 1)
                    else:
                        act.activation(qT[0:CB, 1, :], qk_bank[m][0:CB, :], ACT.Identity,
                                       bias=bias_qkv[0:CB, m:m + 1])
                        act.activation(kT[0:CB, 1, :], qk_bank[m][CB:P, :], ACT.Identity,
                                       bias=bias_qkv[CB:P, m:m + 1]).then_inc(qk_set, 1)
                for t in range(NT):
                    act.wait_ge(v_mm, NT * g + 1 + t)
                    act.copy(vt[:, t, :], v_bank[t][:, 0:C]).then_inc(v_part, 1)

            def half_y(g, t):
                if t == 0:
                    after(act, y_set, NT * g)
                act.wait_ge(y_mm, NT * g + 1 + t)
                act.copy(yh[:, t, :], y_bank[t][:, C:2 * C]).then_inc(y_half[1], 1)

            def exps(g, n):
                act.wait_ge(s_less, 2 * g + 1 + n)
                act.activation(prob[:, HEAD_SETS[n]], prob[:, HEAD_SETS[n]], ACT.Exp).then_inc(p_exp, 1)

            def soft(g):
                half_y(g - 1, 0)
                exps(g + 1, 0)
                half_y(g - 1, 1)
                exps(g + 1, 1)
                half_y(g - 1, 2)

            def mlp1(g, woven):
                act.wait_ge(turned[1], 2 * g + 1)
                act.copy(mA_hi[:], TA2).then_inc(hi_set[1], 1)
                act.wait_ge(turned[1], 2 * g + 2)
                for high_at, _, cols, _ in b_parts:
                    last = act.copy(mB[high_at, cols], TB2[high_at, 0:T // 2])
                last.then_inc(hi_set[1], 1)
                if not isinstance(g, int) or g > 0:
                    half_y(g - 1, NT - 1)
                after(act, y_mm, NT * g)
                for m in range(NH1):
                    if m == 4 and woven:
                        copy_probs(g + 1)
                    act.wait_ge(hid_mm, NH1 * g + 1 + m)
                    act.activation(hid[:, m, :], hid_bank[m], ACT.Gelu,
                                   bias=bias_hid[:, m:m + 1]).then_inc(hid_set, 1)
                    if 0 < m < NH1 - 1:
                        high(g, m - 1)

            act.wait_ge(prep_bias, 2)
            act.wait_ge(pt_zero, 1)
            front(0)
            exps(0, 0)
            exps(0, 1)
            copy_probs(0)
            back(0)
            front(1)
            exps(1, 0)
            exps(1, 1)
            mlp1(0, True)
            with act.Fori(1, G - 1) as g:
                back(g)
                front(g + 1)
                soft(g)
                mlp1(g, True)
            back(G - 1)
            high(G - 2, NH1 - 2)
            high(G - 2, NH1 - 1)
            for t in range(NT - 1):
                half_y(G - 2, t)
            mlp1(G - 1, False)
            high(G - 1, NH1 - 2)
            high(G - 1, NH1 - 1)
            for t in range(NT):
                half_y(G - 1, t)

        @block.vector
        def _(dve):
            scratch = hid[:].rearrange("p m t -> p (m t)")
            gained_qkv = scratch[:, 0:2 * 3 * C].rearrange("p (n c) -> p n c", n=2)
            gained_w1 = scratch[:, 2 * 3 * C:2 * (3 * C + HID)].rearrange("p (n c) -> p n c", n=2)

            def prep_start():
                dve.memset(mhalf[:], -0.5).then_inc(prep_half, 1)
                dve.memset(pT[:].bitcast(mybir.dt.uint32), 0).then_inc(pt_zero, 1)
                dve.wait_ge(pt_zero, 1)

            def prep_qkv_weights():
                dve.wait_ge(consts_in[0], 6 * 16)
                for dst in (qkv_hi, gained_qkv):
                    for n in range(2):
                        for a, b, scale in ((0, P, QSCALE), (P, 2 * P, 1.0), (2 * P, 2 * P + CB, QSCALE),
                                            (2 * P + CB, 3 * C, 1.0)):
                            last = dve.tensor_scalar(dst[:, n, a:b], raw_qkv[:, n, a:b], lncol[:, n:n + 1],
                                                     scale, ALU.mult, ALU.mult)
                last.then_inc(prep_gained, 1)

            def prep_qkv_rest():
                dve.wait_ge(prep_qkv_mm, 1)
                dve.tensor_tensor(bias_qkv[:, 0:4], scores[:, 0, 0:4], bqkv_col[:, 0:4], ALU.add)
                dve.tensor_tensor(bias_qkv[0:CB, 4:5], scores[0:CB, 0, 4:5], bqkv_col[0:CB, 4:5],
                                  ALU.add).then_inc(prep_bias, 1)
                dve.wait_ge(prep_bias, 1)
                dve.tensor_scalar(bias_qkv[:, 0:1], bias_qkv[:, 0:1], QSCALE, None, ALU.mult)
                dve.tensor_scalar(bias_qkv[0:CB, 2:3], bias_qkv[0:CB, 2:3], QSCALE, None, ALU.mult)
                dve.tensor_copy(bv_cols[:, 0, :], bias_qkv[:, 3:4].broadcast_to([P, P]))
                dve.tensor_copy(bv_cols[0:CB, 1, :],
                                bias_qkv[0:CB, 4:5].broadcast_to([CB, P])).then_inc(prep_bias, 1)
                dve.wait_ge(prep_gained, 1)
                dve.tensor_tensor(qkv_lo[:], gained_qkv, qkv_hi[:], ALU.subtract).then_inc(prep_qkv, 1)

            def prep_proj_add():
                dve.wait_ge(prep_proj_mm, 1)
                dve.tensor_tensor(bproj_all[:], bproj_all[:], scores[:, 1, 0:C], ALU.add).then_inc(prep_proj, 1)

            def prep_other_weights():
                dve.wait_ge(consts_in[1], 6 * 16)
                for dst in (w1_hi, gained_w1):
                    for n in range(2):
                        dve.tensor_scalar(dst[:, n, :], raw_w1[:, n, :], lncol[:, 4 + n:5 + n], None, ALU.mult)
                dve.tensor_copy(wp_w[:, :, 0, :], raw_wp[:])
                dve.tensor_copy(w2_w[:, :, 0, :], raw_w2[:]).then_inc(prep_gained, 1)
                dve.wait_ge(prep_gained, 2)
                dve.tensor_tensor(w1_lo[:], gained_w1, w1_hi[:], ALU.subtract)
                dve.tensor_tensor(wp_w[:, :, 1, :], raw_wp[:], wp_w[:, :, 0, :], ALU.subtract)
                dve.tensor_tensor(w2_w[:, :, 1, :], raw_w2[:], w2_w[:, :, 0, :], ALU.subtract).then_inc(prep_rest, 1)

            def prep_hid_add():
                dve.wait_ge(prep_hid_mm, 1)
                dve.tensor_tensor(bias_hid[:], scores[:, 2, 0:NH1], b1_col[:], ALU.add).then_inc(prep_hid, 1)

            def moments(g, n, src):
                for t in range(NT):
                    last = dve.bn_stats(stats[:, n, t, :], src[:, t, :])
                last.then_inc(ln_stats[n], 1)
                wait_alone(dve, ln_stats[n], g + 1)
                for t in range(NT):
                    last = dve.bn_aggr(mv[:, n, t, :], stats[:, n, t, :])
                last.then_inc(ln_mv[n], 1)

            def normalise(g, n, src):
                after(dve, turned[n], 2 * g)
                dve.wait_ge(ln_rstd[n], g + 1)
                for t in range(NT):
                    last = dve.tensor_scalar(xn[:, n, t, :], src[:, t, :], mv[:, n, t, 0:1],
                                             rstd[:, n, t:t + 1], ALU.subtract, ALU.mult)
                last.then_inc(ln_norm[n], 1)
                dve.wait_ge(ln_norm[n], 2 * g + 1)
                dve.tensor_copy(xnB[:, n, :, :], xn[:, n, :, P:C]).then_inc(ln_norm[n], 1)

            def moments1(g):
                dve.wait_ge(x_in, 32 * g + 32)
                moments(g, 0, xin)

            def copy_probs(g):
                for n in range(3):
                    dve.wait_ge(pt_mm, 3 * g + 1 + n)
                    dve.tensor_copy(pT[WT:P, 2 * n:2 * n + 2, :, WT:P].rearrange("p h t q -> p (h t) q"),
                                    pt_bank[n][WT:P, :].rearrange("p (x q) -> p x q", q=WT)).then_inc(pt_set[1], 1)

            def back(g):
                for n, (bank, h, d) in enumerate((
                    (PV0, attA_hi[:], attA_lo[:]), (PV1[0:CB, :], attB[0:CB, :], attB[CB:P, :]),
                )):
                    dve.wait_ge(att_split[0], 2 * g + 1 + n)
                    for dst, src, high in zip(ww_cols(d), win_cols(bank), ww_cols(h)):
                        last = dve.tensor_tensor(dst, src, high, ALU.subtract)
                    last.then_inc(att_split[1], 1)

            def residual(g):
                after(dve, x2b_set, g)
                dve.wait_ge(xres_set, g + 1)
                pairs = [slice(2 * n, 2 * n + 2) for n in range(2)]
                for n, t in enumerate(pairs):
                    dve.wait_ge(proj_mm, 2 * g + 1 + n)
                    dve.tensor_tensor(x2[:, t, :], xres[:, t, :], proj_bank[:, t, 0:C], ALU.add).then_inc(x2_part, 1)
                for n, t in enumerate(pairs):
                    dve.wait_ge(x2_part, 2 * g + 1 + n)
                    dve.tensor_tensor(x2[:, t, :], x2[:, t, :], proj_bank[:, t, C:2 * C],
                                      ALU.add).then_inc(x2_set, 1)
                dve.wait_ge(x2_set, 2 * g + 2)
                moments(g, 1, x2)

            def low1(g):
                dve.wait_ge(hi_set[0], 2 * g + 1)
                for (d, s, h) in zip(win_cols(hA_lo[:]), ww_cols(TA1), win_cols(hA_hi[:])):
                    last = dve.tensor_tensor(d, s, h, ALU.subtract)
                last.then_inc(lo_set[0], 1)
                dve.wait_ge(hi_set[0], 2 * g + 2)
                for high_at, low_at, _, rows in b_parts:
                    for d, s, h in zip(win_cols(hB[low_at, :], rows), ww_cols(TB1[high_at, 0:T // 2]),
                                       win_cols(hB[high_at, :], rows)):
                        last = dve.tensor_tensor(d, s, h, ALU.subtract)
                last.then_inc(lo_set[0], 1)

            def values(g, t):
                dve.wait_ge(v_part, NT * g + 1 + t)
                dve.tensor_tensor(vt[:, t, :], vt[:, t, :], v_bank[t][:, C:2 * C], ALU.add).then_inc(v_set, 1)

            def prob_rows(n):
                hs = HEAD_SETS[n]
                rows = slice(hs.start * 4, hs.stop * 4)
                p3 = prob[:, hs, :].rearrange("p h (w k) -> p (h w) k", k=WT)
                return rows, p3

            def biased(g, n):
                last_row = ((g & 7) + 1) >> 3
                src = (scores[:, 0:4, 0:4 * WT], scores[:, 0:2, 4 * WT:8 * WT])[n]
                dve.wait_ge(s_mm, 2 * g + 1 + n)
                dve.tensor_tensor(prob[:, HEAD_SETS[n], :], src, bias_att[:, last_row, HEAD_SETS[n], :],
                                  ALU.add).then_inc(s_biased, 1)

            def less_max(g, n):
                rows, p3 = prob_rows(n)
                dve.wait_ge(s_biased, 2 * g + 1 + n)
                dve.tensor_reduce(pmax[:, rows], p3, AX_X, ALU.max).then_inc(s_max, 1)
                dve.wait_ge(s_max, 2 * g + 1 + n)
                dve.tensor_tensor(p3, p3, pmax[:, rows].unsqueeze(2).broadcast_to([P, rows.stop - rows.start, WT]),
                                  ALU.subtract).then_inc(s_less, 1)

            def sums(g, n):
                rows, p3 = prob_rows(n)
                dve.wait_ge(p_exp, 2 * g + 1 + n)
                dve.tensor_reduce(psum_[:, rows], p3, AX_X, ALU.add).then_inc(p_sum, 1)
                dve.wait_ge(p_sum, 2 * g + 1 + n)
                dve.reciprocal(prec[:, rows], psum_[:, rows]).then_inc(p_rec, 1)

            def mlp_lo_a(g):
                dve.wait_ge(hi_set[1], 2 * g + 1)
                dve.tensor_tensor(mA_lo[:], TA2, mA_hi[:], ALU.subtract).then_inc(lo_set[1], 1)

            def mlp_lo_b(g):
                dve.wait_ge(hi_set[1], 2 * g + 2)
                for high_at, low_at, cols, _ in b_parts:
                    last = dve.tensor_tensor(mB[low_at, cols], TB2[high_at, 0:T // 2], mB[high_at, cols],
                                             ALU.subtract)
                last.then_inc(lo_set[1], 1)

            def result(g, t):
                if t == 0:
                    dve.wait_ge(x2b_set, g + 1)
                    after(dve, y_out, 32 * g)
                wait_alone(dve, y_half[1], NT * g + 1 + t)
                dve.tensor_tensor(yt[:, t, :], x2b[:, t, :], y_bank[t][:, 0:C], ALU.add).then_inc(y_half[0], 1)

            def steps(g, first=False, last=False, x_after=True):
                back(g)
                if not last:
                    low1(g + 1)
                residual(g)
                if last:
                    normalise(g, 1, x2)
                else:
                    values(g + 1, 0)
                    normalise(g, 1, x2)
                    values(g + 1, 1)
                    biased(g + 1, 0)
                    values(g + 1, 2)
                    values(g + 1, 3)
                    less_max(g + 1, 0)
                    biased(g + 1, 1)
                    less_max(g + 1, 1)
                    sums(g + 1, 0)
                if not first:
                    result(g - 1, 0)
                mlp_lo_a(g)
                if not first:
                    result(g - 1, 1)
                mlp_lo_b(g)
                if not first:
                    result(g - 1, 2)
                if not last:
                    sums(g + 1, 1)
                if not first:
                    result(g - 1, 3)
                if x_after and not last:
                    moments1(g + 2)
                if not last:
                    copy_probs(g + 1)
                if x_after and not last:
                    normalise(g + 2, 0, xin)

            prep_start()
            moments1(0)
            prep_qkv_weights()
            normalise(0, 0, xin)
            prep_qkv_rest()
            low1(0)
            prep_proj_add()
            prep_other_weights()
            values(0, 0)
            values(0, 1)
            dve.wait_ge(prep_att, 1)
            biased(0, 0)
            values(0, 2)
            values(0, 3)
            less_max(0, 0)
            biased(0, 1)
            less_max(0, 1)
            sums(0, 0)
            sums(0, 1)
            prep_hid_add()
            moments1(1)
            normalise(1, 0, xin)
            copy_probs(0)
            steps(0, first=True)
            with dve.Fori(1, G - 2) as g:
                steps(g)
            steps(G - 2, x_after=False)
            steps(G - 1, last=True)
            for m in range(1, NH1, 2):
                dve.wait_ge(hid_split[0], NH1 * (G - 1) + m + 1)
                dve.tensor_tensor(hid_lo[:, m, :], hid[:, m, :], hid_hi[:, m, :],
                                  ALU.subtract).then_inc(hid_split[1], 1)
            for t in range(NT):
                result(G - 1, t)

        @block.gpsimd
        def _(pool):
            def scale(g, n):
                wait_alone(pool, ln_mv[n], g + 1)
                pool.tensor_scalar(veps[:, n, :], mv[:, n, :, 1], EPS, None, ALU.add).then_inc(ln_eps[n], 1)
                pool.wait_ge(ln_eps[n], g + 1)
                pool.tensor_tensor(rstd[:, n, :], veps[:, n, :], mhalf[:], ALU.pow).then_inc(ln_rstd[n], 1)

            def keep_x(g):
                pool.wait_ge(x_in, 32 * g + 32)
                after(pool, x2_set, 2 * g)
                pool.tensor_tensor(xres[:], xin[:], bproj_all[:].unsqueeze(1).broadcast_to([P, NT, C]),
                                   ALU.add).then_inc(xres_set, 1)

            def keep_x2(g):
                after(pool, y_set, NT * g)
                pool.tensor_tensor(x2b[:], x2[:], b2_all[:].unsqueeze(1).broadcast_to([P, NT, C]),
                                   ALU.add).then_inc(x2b_set, 1)

            def probs(g, n=None):
                for n in (0, 1) if n is None else (n,):
                    hs = HEAD_SETS[n]
                    rows = slice(hs.start * 4, hs.stop * 4)
                    p3 = prob[:, hs, :].rearrange("p h (w k) -> p (h w) k", k=WT)
                    pool.wait_ge(p_rec, 2 * g + 1 + n)
                    pool.tensor_tensor(p3, p3, prec[:, rows].unsqueeze(2).broadcast_to([P, rows.stop - rows.start, WT]),
                                       ALU.mult).then_inc(p_norm, 1)

            def add_half(g, t):
                pool.wait_ge(y_half[0], NT * g + 1 + t)
                pool.tensor_tensor(yt[:, t, :], yt[:, t, :], yh[:, t, :], ALU.add).then_inc(y_set, 1)

            def low(g, step=1):
                for m in range(0, NH1, step):
                    pool.wait_ge(hid_split[0], NH1 * g + m + 1)
                    pool.tensor_tensor(hid_lo[:, m, :], hid[:, m, :], hid_hi[:, m, :],
                                       ALU.subtract).then_inc(hid_split[1], 1)

            pool.wait_ge(prep_half, 1)
            scale(0, 0)
            pool.wait_ge(consts_in[1], 6 * 16)
            for kind in range(2):
                for h in range(HEADS):
                    last = pool.tensor_tensor(bias_att[:, kind, h, :], rel_sb[:, h, :],
                                              mask_sb[:, kind, :], ALU.add)
            last.then_inc(prep_att, 1)
            pool.wait_ge(prep_proj, 1)
            keep_x(0)
            scale(1, 0)
            probs(0)
            scale(0, 1)
            keep_x(1)
            probs(1)
            scale(2, 0)
            keep_x2(0)
            low(0)
            with pool.Fori(1, G - 2) as g:
                scale(g, 1)
                keep_x(g + 1)
                probs(g + 1, 0)
                add_half(g - 1, 0)
                add_half(g - 1, 1)
                probs(g + 1, 1)
                add_half(g - 1, 2)
                add_half(g - 1, 3)
                scale(g + 2, 0)
                keep_x2(g)
                low(g)
            scale(G - 2, 1)
            keep_x(G - 1)
            for t in range(NT):
                add_half(G - 3, t)
            probs(G - 1)
            keep_x2(G - 2)
            low(G - 2)
            scale(G - 1, 1)
            for t in range(NT):
                add_half(G - 2, t)
            keep_x2(G - 1)
            low(G - 1, 2)
            for t in range(NT):
                add_half(G - 1, t)


def _token(win_kind):
    i, j = np.meshgrid(ROWS, np.arange(WIN), indexing="ij")
    if win_kind == "wrapped":
        j = (j + SHIFT) % WIN
    return i.ravel(), j.ravel()


def _places():
    iq = np.zeros((P, 4 * WT), np.int64)
    jq, ik, jk, wrap = iq.copy(), iq.copy(), iq.copy(), np.zeros((P, 4 * WT), bool)
    for tp in range(2):
        for tt in range(2):
            for w in range(2):
                last = 4 * tt + 2 * tp + w == NWIN - 1
                i, j = _token("wrapped" if last else "regular")
                rows, cols = slice(WT * tp, WT * (tp + 1)), slice((2 * tt + w) * WT, (2 * tt + w + 1) * WT)
                iq[rows, cols], jq[rows, cols] = i[:, None], j[:, None]
                ik[rows, cols], jk[rows, cols] = i[None, :], j[None, :]
                wrap[rows, cols] = last
    return iq, jq, ik, jk, wrap


def _lay_out(inputs):
    a = {k: np.asarray(v) for k, v in inputs.items()}
    f = np.float32
    p = "L0_conv_"

    def two_parts(w):
        return np.ascontiguousarray(np.stack([w[:P], np.concatenate([w[P:], w[P:]])], 1))

    def two_cols(v):
        return np.stack([v[:P], np.concatenate([v[P:], v[P:]])], 1)

    order = np.concatenate([np.arange(0, P), np.arange(C, C + P), np.arange(P, C), np.arange(C + P, 2 * C),
                            np.arange(2 * C, 3 * C)])
    bq = a[p + "b_qkv"][order]
    zeros = np.zeros(CB, f)
    bqkv = np.stack([bq[0:P], bq[P:2 * P], bq[2 * P:3 * P], bq[2 * C:2 * C + P],
                     np.concatenate([bq[2 * C + P:], zeros])], 1)
    ln = np.concatenate([two_cols(a[p + n]) for n in ("g1", "b1", "g2", "b2")], 1)
    iq, jq, ik, jk, wrap = _places()
    rel = a[p + "rel_pos"][:, iq - ik + WIN - 1, jq - jk + WIN - 1].transpose(1, 0, 2)
    across_cols = wrap & ((jq < SHIFT) != (jk < SHIFT))
    across_rows = (iq < SHIFT) != (ik < SHIFT)
    mask = np.stack([across_cols, across_cols | across_rows], 1).astype(f) * f(MASKED)
    c = np.ascontiguousarray
    return {
        "x": c(a["x"]), "wqkv": two_parts(a[p + "w_qkv"][:, order]), "bqkv": c(bqkv), "ln": c(ln),
        "rel": c(rel), "mask": c(mask), "wproj": two_parts(a[p + "w_proj"]), "bproj": c(a[p + "b_proj"]),
        "w1": two_parts(a[p + "w_mlp1"]), "b1": c(a[p + "b_mlp1"].reshape(NH1, P).T),
        "w2": c(a[p + "w_mlp2"].reshape(NH1, P, C).transpose(1, 0, 2)), "b2": c(a[p + "b_mlp2"]),
        "ident": np.eye(P, dtype=f),
    }


def kernel(**inputs):
    import concourse.bacc as bacc
    from concourse.bass_utils import run_bass_kernel_spmd

    arrays = _lay_out(inputs)
    nc = bacc.Bacc("TRN2", target_bir_lowering=False, num_devices=1)
    args = {k: nc.dram_tensor(f"in_{k}", v.shape, F32, kind="ExternalInput").ap() for k, v in arrays.items()}
    out = nc.dram_tensor("out", (B, H, W, C), F32, kind="ExternalOutput").ap()
    swin_block(nc, out=out, **args)
    r = run_bass_kernel_spmd(nc, [{f"in_{k}": v for k, v in arrays.items()}], core_ids=[0])
    return r.results[0]["out"]
```
